# Optimizing a Trainium2 kernel written in Bass

```python
import numpy as np
import jax
import jax.numpy as jnp

def _softmax(x, axis=-1):
    return jax.nn.softmax(x, axis=axis)

def _gelu(x):
    return jax.nn.gelu(x, approximate=True)

def _silu(x):
    return jax.nn.silu(x)

def _sigmoid(x):
    return jax.nn.sigmoid(x)

def _layernorm(x, axis=-1, eps=1e-05):
    m = jnp.mean(x, axis=axis, keepdims=True)
    v = jnp.var(x, axis=axis, keepdims=True)
    return (x - m) / jnp.sqrt(v + eps)

def _scatter_add(tgt, idx, src, axis=0):
    return tgt.at[idx].add(src)

def _segment_sum(src, seg, n):
    return jax.ops.segment_sum(src, seg, n)
kernel_name = 'mk_hybrid_d1_jaxref_r8_6236e2'

def setup_inputs(seed: int=0):
    np.random.seed(seed)
    _w = jnp.asarray

    def _L0_attn_a_setup():
        import jax, jax.numpy as jnp
        import numpy as np
        ROPE_THETA = 10000.0
        N_HEAD = 16

        def _rope(x, theta):
            T, D = (x.shape[-2], x.shape[-1])
            pos = jnp.arange(T, dtype=jnp.float32)
            inv_freq = 1.0 / theta ** (jnp.arange(0, D, 2, dtype=jnp.float32) / D)
            freqs = pos[:, None] * inv_freq[None, :]
            cos = jnp.cos(freqs).astype(x.dtype)[None, None]
            sin = jnp.sin(freqs).astype(x.dtype)[None, None]
            x_even = x[..., ::2]
            x_odd = x[..., 1::2]
            rot = jnp.stack((x_even * cos - x_odd * sin, x_even * sin + x_odd * cos), axis=-1)
            return rot.reshape(x.shape)
        key = jax.random.key(seed)
        ks = jax.random.split(key, 5)
        B, T, E = (4, 256, 128)
        s = 0.02
        return {'x': jax.random.normal(ks[0], (B, T, E), jnp.float32), 'Wqkv': jax.random.normal(ks[1], (E, 3 * E), jnp.float32) * s, 'bqkv': jax.random.normal(ks[2], (3 * E,), jnp.float32) * s, 'Wproj': jax.random.normal(ks[3], (E, E), jnp.float32) * s, 'bproj': jax.random.normal(ks[4], (E,), jnp.float32) * s}
    _L0_attn_a_in = _L0_attn_a_setup()

    def _L0_attn_b_setup():
        import jax, jax.numpy as jnp
        import numpy as np
        B, T, C = (64, 32, 128)
        N_HEAD, HEAD_SIZE, KV_RANK = (16, 64, 128)
        BLOCK_SIZE = 32
        key = jax.random.key(seed)
        ks = jax.random.split(key, 5)
        HD = N_HEAD * HEAD_SIZE

        def init(k, shape):
            fan_in = shape[0]
            bound = 1.0 / np.sqrt(fan_in)
            return jax.random.uniform(k, shape, jnp.float32, -bound, bound)
        return {'x': jax.random.normal(ks[0], (B, T, C), jnp.float32), 'w_kv_down': init(ks[1], (C, KV_RANK)), 'w_kv_up': init(ks[2], (KV_RANK, 2 * HD)), 'w_q': init(ks[3], (C, HD)), 'w_out': init(ks[4], (HD, C))}
    _L0_attn_b_in = _L0_attn_b_setup()

    def _L0_ffn_setup():
        import jax, jax.numpy as jnp
        import numpy as np
        DIM = 128
        DEPTH = 7
        PAR = 8
        N_NODES = 2 ** (DEPTH + 1) - 1
        WIDTH = PAR * N_NODES
        key = jax.random.key(seed)
        k1, k2, k3, k4 = jax.random.split(key, 4)
        init_k = float(np.sqrt(1.0 / DIM))
        init_k2 = float(np.sqrt(1.0 / ((DEPTH + 1) * PAR)))
        oldx = jax.random.normal(k1, (4, 256, DIM), dtype=jnp.float32)
        W_in = jax.random.uniform(k2, (WIDTH, DIM), jnp.float32, -init_k, init_k)
        b_in = jax.random.uniform(k3, (WIDTH,), jnp.float32, -init_k, init_k)
        W_out = jax.random.uniform(k4, (DIM, WIDTH), jnp.float32, -init_k2, init_k2)
        return {'oldx': oldx, 'W_in': W_in, 'b_in': b_in, 'W_out': W_out}
    _L0_ffn_in = _L0_ffn_setup()
    _d = {'L0_attn_a_x': _L0_attn_a_in['x'], 'L0_attn_a_Wqkv': _L0_attn_a_in['Wqkv'], 'L0_attn_a_bqkv': _L0_attn_a_in['bqkv'], 'L0_attn_a_Wproj': _L0_attn_a_in['Wproj'], 'L0_attn_a_bproj': _L0_attn_a_in['bproj'], 'L0_attn_b_w_kv_down': _L0_attn_b_in['w_kv_down'], 'L0_attn_b_w_kv_up': _L0_attn_b_in['w_kv_up'], 'L0_attn_b_w_q': _L0_attn_b_in['w_q'], 'L0_attn_b_w_out': _L0_attn_b_in['w_out'], 'L0_ffn_W_in': _L0_ffn_in['W_in'], 'L0_ffn_b_in': _L0_ffn_in['b_in'], 'L0_ffn_W_out': _L0_ffn_in['W_out']}
    _x0 = _d['L0_attn_a_x']
    _d['L0_attn_a_x'] = jax.random.normal(jax.random.fold_in(jax.random.key(seed), 1), (1, 2048, 128), dtype=_x0.dtype)
    del _x0
    return _d

def reference(L0_attn_a_x, L0_attn_a_Wqkv, L0_attn_a_bqkv, L0_attn_a_Wproj, L0_attn_a_bproj, L0_attn_b_w_kv_down, L0_attn_b_w_kv_up, L0_attn_b_w_q, L0_attn_b_w_out, L0_ffn_W_in, L0_ffn_b_in, L0_ffn_W_out):

    def _L0_attn_a_ref(x, Wqkv, bqkv, Wproj, bproj):
        import jax, jax.numpy as jnp
        import numpy as np
        ROPE_THETA = 10000.0
        N_HEAD = 16

        def _rope(x, theta):
            T, D = (x.shape[-2], x.shape[-1])
            pos = jnp.arange(T, dtype=jnp.float32)
            inv_freq = 1.0 / theta ** (jnp.arange(0, D, 2, dtype=jnp.float32) / D)
            freqs = pos[:, None] * inv_freq[None, :]
            cos = jnp.cos(freqs).astype(x.dtype)[None, None]
            sin = jnp.sin(freqs).astype(x.dtype)[None, None]
            x_even = x[..., ::2]
            x_odd = x[..., 1::2]
            rot = jnp.stack((x_even * cos - x_odd * sin, x_even * sin + x_odd * cos), axis=-1)
            return rot.reshape(x.shape)
        B, T, E = x.shape
        H = N_HEAD
        D = E // H
        qkv = x @ Wqkv + bqkv
        q, k, v = jnp.split(qkv, 3, axis=-1)
        q = q.reshape(B, T, H, D).transpose(0, 2, 1, 3)
        k = k.reshape(B, T, H, D).transpose(0, 2, 1, 3)
        v = v.reshape(B, T, H, D).transpose(0, 2, 1, 3)
        q = _rope(q, ROPE_THETA)
        k = _rope(k, ROPE_THETA)
        scores = jnp.einsum('bhqd,bhkd->bhqk', q, k) * D ** (-0.5)
        causal = jnp.tril(jnp.ones((T, T), dtype=bool))
        scores = jnp.where(causal[None, None], scores, -jnp.inf)
        weights = jax.nn.softmax(scores, axis=-1)
        out = jnp.einsum('bhqk,bhkd->bhqd', weights, v)
        out = out.transpose(0, 2, 1, 3).reshape(B, T, E)
        return out @ Wproj + bproj

    def _L0_attn_b_ref(x, w_kv_down, w_kv_up, w_q, w_out):
        import jax, jax.numpy as jnp
        import numpy as np
        B, T, C = (64, 32, 128)
        N_HEAD, HEAD_SIZE, KV_RANK = (16, 64, 128)
        BLOCK_SIZE = 32
        Bx, Tx, Cx = x.shape
        HD = N_HEAD * HEAD_SIZE
        latent_kv = x @ w_kv_down
        kv = latent_kv @ w_kv_up
        k, v = (kv[..., :HD], kv[..., HD:])
        k = k.reshape(Bx, Tx, N_HEAD, HEAD_SIZE)
        v = v.reshape(Bx, Tx, N_HEAD, HEAD_SIZE)
        q = (x @ w_q).reshape(Bx, Tx, N_HEAD, HEAD_SIZE)
        scale = HEAD_SIZE ** (-0.5)
        att = jnp.einsum('bqhd,bkhd->bhqk', q, k) * scale
        causal = jnp.tril(jnp.ones((Tx, Tx), dtype=bool))
        att = jnp.where(causal, att, -jnp.inf)
        att = jax.nn.softmax(att, axis=-1)
        y = jnp.einsum('bhqk,bkhd->bqhd', att, v)
        y = y.reshape(Bx, Tx, HD)
        return y @ w_out

    def _L0_ffn_ref(oldx, W_in, b_in, W_out):
        import jax, jax.numpy as jnp
        import numpy as np
        DIM = 128
        DEPTH = 7
        PAR = 8
        N_NODES = 2 ** (DEPTH + 1) - 1
        WIDTH = PAR * N_NODES
        x = oldx.reshape(-1, DIM)
        B = x.shape[0]
        logits = x @ W_in.T + b_in
        decisions = (logits > 0).astype(jnp.int32).reshape(B, PAR, N_NODES)
        acts = jax.nn.silu(logits).reshape(B, PAR, N_NODES)
        current = jnp.zeros((B, PAR), dtype=jnp.int32)
        dmap = jax.nn.one_hot(current, N_NODES, dtype=acts.dtype)
        for d in range(DEPTH):
            cur_platform = 2 ** d - 1
            next_platform = 2 ** (d + 1) - 1
            moves = jnp.take_along_axis(decisions, current[..., None], axis=2)[..., 0]
            current = (current - cur_platform) * 2 + moves + next_platform
            dmap = dmap + jax.nn.one_hot(current, N_NODES, dtype=acts.dtype)
        masked = acts * jax.lax.stop_gradient(dmap)
        out = masked.reshape(B, WIDTH) @ W_out.T
        return out.reshape(oldx.shape)
    x = L0_attn_a_x
    x = x + _L0_attn_a_ref(_layernorm(x, axis=-1), L0_attn_a_Wqkv, L0_attn_a_bqkv, L0_attn_a_Wproj, L0_attn_a_bproj)
    x = x + _L0_ffn_ref(_layernorm(x, axis=-1), L0_ffn_W_in, L0_ffn_b_in, L0_ffn_W_out)
    x = x + _L0_attn_b_ref(_layernorm(x, axis=-1), L0_attn_b_w_kv_down, L0_attn_b_w_kv_up, L0_attn_b_w_q, L0_attn_b_w_out)
    x = x + _L0_ffn_ref(_layernorm(x, axis=-1), L0_ffn_W_in, L0_ffn_b_in, L0_ffn_W_out)
    return x

_drawn_inputs = setup_inputs


def setup_inputs(seed=0):
    import zlib

    import numpy as np

    out = dict(_drawn_inputs(seed))
    spreads = {}
    factors = {'L0_attn_a_Wqkv': 3.117, 'L0_attn_b_w_q': 3.457}
    for name, (base, spread) in spreads.items():
        noise = np.random.default_rng([zlib.crc32(name.encode()), seed]).standard_normal(out[name].shape)
        drawn = base * np.exp(spread * noise) if base else spread * noise
        out[name] = jnp.asarray(drawn.astype(out[name].dtype))
    for name, factor in factors.items():
        out[name] = (out[name] * factor).astype(out[name].dtype)
    return out
```

```python
from contextlib import ExitStack

import concourse.bass as bass
from concourse import mybir

F32 = mybir.dt.float32
BF16 = mybir.dt.bfloat16
ALU = mybir.AluOpType
ACT = mybir.ActivationFunctionType
AX = mybir.AxisListType

P = 128
T = 2048
E = 128
NT = T // P
C = 512
NC = T // C
TPC = C // P
H = 16
DA = E // H
DB = 64
EPS = 1e-5
NEG = -1e30
LOWEST = -3e38
TREES = 8
DEPTH = 7
PARTS = 3

UNITS = [(j, kt) for j in range(NC) for kt in range(TPC * (j + 1))]
PIECES = [(i, ch) for i in range(NT) for ch in range(i // TPC + 1)]
NU = len(UNITS)
NP = len(PIECES)
LAST_UNIT = {j: max(n for n, u in enumerate(UNITS) if u[0] == j) for j in range(NC)}
FIRST_MAX, END_MAX = 8, 36
TURN = 37
PV_LAG = 2
NPB = 4


def pieces_at(n):
    span = END_MAX - FIRST_MAX
    if not FIRST_MAX <= n < END_MAX:
        return range(0)
    return range((n - FIRST_MAX) * NP // span, (n + 1 - FIRST_MAX) * NP // span)


PAIRS = [(0, 0), (0, 1), (1, 0), (1, 1), (0, 2), (2, 0)]


class Arena:

    def __init__(self, whole):
        self.whole, self.at = whole, 0

    def take(self, words):
        a = self.whole[:, self.at:self.at + words]
        self.at += words
        return a

    def f32(self, *dims):
        n = 1
        for d in dims:
            n *= d
        return shaped(self.take(n), dims)

    def bf16(self, *dims):
        n = 1
        for d in dims:
            n *= d
        return shaped(self.take(n // 2).bitcast(BF16), dims)


def shaped(ap, dims):
    if len(dims) == 1:
        return ap
    if len(dims) == 2:
        return ap.rearrange("p (a b) -> p a b", b=dims[1])
    return ap.rearrange("p (a b c) -> p a b c", b=dims[1], c=dims[2])


class Chain:

    def __init__(self, eng, sem):
        self.eng, self.sem, self.n = eng, sem, 0

    def link(self, ins):
        ins.then_inc(self.sem, 1)
        self.n += 1
        self.eng.wait_ge(self.sem, self.n)


class Norm:

    def __init__(self, name, sem, g):
        self.g = g
        self.var_ready = sem(f"{name}_var_ready")
        self.std_ready = sem(f"{name}_std_ready")
        self.rows_ready = sem(f"{name}_rows_ready")
        self.turned = sem(f"{name}_turned")
        self.xT_ready = sem(f"{name}_xT_ready")
        self.own = sem(f"{name}_own")

    def vector(self, nc, dve):
        g, chain = self.g, Chain(dve, self.own)
        for t in range(NT):
            last = nc.vector.bn_stats(g.stats[:, t, :], g.x[:, t, :])
        chain.link(last)
        for t in range(NT):
            last = nc.vector.bn_aggr(g.mv[:, t, :], g.stats[:, t, :])
        chain.link(last)
        nc.vector.tensor_scalar(g.ve, g.mv[:, :, 1], EPS, None, ALU.add).then_inc(self.var_ready, 1)
        dve.wait_ge(self.std_ready, 1)
        chain.link(nc.vector.reciprocal(g.rstd, g.std))
        for c in range(NC):
            if c >= 2:
                dve.wait_ge(self.turned, c - 1)
            for t in range(TPC):
                n = TPC * c + t
                last = nc.vector.tensor_scalar(g.xn[:, c % 2, t * P:(t + 1) * P], g.x[:, n, :],
                                               g.mv[:, n, 0:1], g.rstd[:, n:n + 1],
                                               ALU.subtract, ALU.mult)
            last.then_inc(self.rows_ready, 1)

    def scalar(self, nc, act):
        g = self.g
        act.wait_ge(self.var_ready, 1)
        nc.scalar.activation(g.std, g.ve, ACT.Sqrt).then_inc(self.std_ready, 1)
        for c in range(NC):
            act.wait_ge(self.turned, c + 1)
            nc.scalar.activation(g.xnT[:, c * C:(c + 1) * C], g.bank[c % 2][:, :], ACT.Copy)\
                .then_inc(self.xT_ready, 1)

    def tensor(self, nc, pe):
        g = self.g
        for c in range(NC):
            pe.wait_ge(self.rows_ready, c + 1)
            if c >= 2:
                pe.wait_ge(self.xT_ready, c - 1)
            for t in range(TPC):
                last = nc.tensor.transpose(g.bank[c % 2][:, t * P:(t + 1) * P],
                                           g.xn[:, c % 2, t * P:(t + 1) * P], g.ident)
            last.then_inc(self.turned, 1)


class Attention:

    ROWS = None
    ST_CREDIT = 1

    def __init__(self, name, sem, g):
        self.g = g
        self.st_ready = sem(f"{name}_scores_ready")
        self.exp_done = sem(f"{name}_exp_done")
        self.pv_done = sem(f"{name}_pv_done")
        self.ot_taken = sem(f"{name}_ot_taken")
        self.tr_ready = sem(f"{name}_tr_ready")
        self.norm_done = sem(f"{name}_norm_done")
        self.mx_ready = sem(f"{name}_mx_ready")
        self.mx_done = sem(f"{name}_mx_done")
        self.negm_ready = sem(f"{name}_negm_ready")
        self.mt_ready = sem(f"{name}_mt_ready")
        self.mt_taken = sem(f"{name}_mt_taken")
        self.rows_in = sem(f"{name}_rows_in")
        self.own = sem(f"{name}_own")
        self.consts = sem(f"{name}_consts")

    def vector_credits(self, nc):
        nc.vector.sem_inc(self.norm_done, 2)
        nc.vector.sem_inc(self.ot_taken, 2)
        nc.vector.sem_inc(self.mx_done, 2)
        nc.vector.sem_inc(self.mt_taken, 1)

    def vector_step(self, nc, dve, s, main, prep):
        g, D, b = self.g, self.D, self.parity(s)
        for n in range(NU):
            if prep:
                hp = s + 1
                for m in pieces_at(n):
                    i, ch = PIECES[m]
                    w = self.piece_width(m)
                    dve.wait_ge(self.mx_ready, hp * NP + m + 1)
                    nc.vector.tensor_reduce(g.mpart[:, i, ch:ch + 1], self.sm[m % 2][:, 0:w],
                                            axis=AX.X, op=ALU.max).then_inc(self.mx_done, 1)
                    if m == NP - 1:
                        dve.wait_ge(self.mx_done, hp * NP + NP + 2)
                        nc.vector.tensor_reduce(g.negm, g.mpart, axis=AX.X, op=ALU.max,
                                                negate=True).then_inc(self.negm_ready, 1)
                if n == TURN:
                    dve.wait_ge(self.mt_ready, hp + 1)
                    dve.wait_ge(self.rows_in, self.ROWS * (hp + 1))
                    self.take_rows(nc, dve, hp)
            if main:
                self.for_ends(n, PV_LAG, lambda j: self.take_chunk(nc, dve, s, j))
                self.for_ends(n, PV_LAG + 1, lambda j: self.normalise(nc, dve, s, j))
        if main:
            self.take_chunk(nc, dve, s, NC - 1)
            self.normalise(nc, dve, s, NC - 1)

    def for_ends(self, n, lag, do):
        for j in range(NC - 1):
            if n - lag == LAST_UNIT[j]:
                do(j)

    def take_chunk(self, nc, dve, s, j):
        R = self.D + 2
        dve.wait_ge(self.pv_done, s * NU + LAST_UNIT[j] + 1 + NPB)
        dve.wait_ge(self.tr_ready, s * NC + j + 1)
        nc.vector.tensor_copy(self.g.ot[0:R, j % 2, :], self.pv[j % 2][0:R, :]).then_inc(self.ot_taken, 1)

    def normalise(self, nc, dve, s, j):
        g, D = self.g, self.D
        pv = self.tr
        dve.wait_ge(self.tr_ready, s * NC + j + 3)
        dve.wait_ge(self.norm_done, s * NC + j + 1)
        nc.vector.reciprocal(g.rcp[:, j % 2, :], pv[:, :, D]).then_inc(self.own, 1)
        dve.wait_ge(self.own, self.own_count(s, j))
        nc.vector.tensor_tensor(self.att[:, TPC * j:TPC * (j + 1), bass.ds(s * D, D)], pv[:, :, 0:D],
                                g.rcp[:, j % 2, :].unsqueeze(2).to_broadcast([P, TPC, D]),
                                ALU.mult).then_inc(self.norm_done, 1)

    def own_count(self, s, j):
        return s * NC + j + 1

    def scalar_credits(self, nc):
        nc.scalar.sem_inc(self.exp_done, 2)

    def scalar_step(self, nc, act, s, main, prep):
        g, b = self.g, self.parity(s)
        for n, (j, kt) in enumerate(UNITS):
            off = max(0, kt - TPC * j) * P
            if main:
                act.wait_ge(self.st_ready, s * NU + n + 1 + self.ST_CREDIT)
                act.wait_ge(self.pv_done, s * NU + n + 1)
                nc.scalar.activation(g.pb[:, n % NPB, off:C], self.st[n % 2][:, off:C], ACT.Exp,
                                     scale=self.D ** -0.5).then_inc(self.exp_done, 1)
            if prep:
                self.scalar_prepare(nc, act, s, n)

    def tensor_credits(self, nc):
        nc.tensor.sem_inc(self.st_ready, self.ST_CREDIT)
        nc.tensor.sem_inc(self.pv_done, NPB)
        nc.tensor.sem_inc(self.tr_ready, 2)

    def piece_width(self, m):
        i, ch = PIECES[m]
        return min(C, (i + 1) * P - ch * C)

    def tensor_step(self, nc, pe, s, main, prep):
        g, b = self.g, self.parity(s)
        for n, (j, kt) in enumerate(UNITS):
            if main:
                if n == 0:
                    pe.wait_ge(self.rows_in, self.ROWS * (s + 2))
                off = max(0, kt - TPC * j) * P
                pe.wait_ge(self.exp_done, s * NU + n + 1)
                out = self.st[n % 2]
                mm = nc.tensor.matmul(out[:, off:C], self.k_main[b][:, kt * P:(kt + 1) * P],
                                      self.q_main[b][:, j * C + off:(j + 1) * C],
                                      start=True, stop=kt < TPC * j)
                if kt >= TPC * j:
                    mm = nc.tensor.matmul(out[:, off:off + P], g.identb, g.mask_kq,
                                          start=False, stop=True)
                mm.then_inc(self.st_ready, 1)
            if prep:
                hp = s + 1
                self.tensor_prepare(nc, pe, s, n)
                for m in pieces_at(n):
                    if m == 0:
                        self.wait_operands(pe, hp)
                    i, ch = PIECES[m]
                    w = self.piece_width(m)
                    pe.wait_ge(self.mx_done, hp * NP + m + 1)
                    out = self.sm[m % 2]
                    last = ch == i // TPC
                    mm = nc.tensor.matmul(out[:, 0:w], self.q_max[1 - b][:, i * P:(i + 1) * P],
                                          self.k_max[1 - b][:, ch * C:ch * C + w],
                                          start=True, stop=not last)
                    if last:
                        mm = nc.tensor.matmul(out[:, w - P:w], g.identb, g.mask_qk,
                                              start=False, stop=True)
                    mm.then_inc(self.mx_ready, 1)
                if n == TURN:
                    pe.wait_ge(self.negm_ready, hp + 1)
                    pe.wait_ge(self.mt_taken, hp + 1)
                    self.wait_turn_bank(pe, hp)
                    nc.tensor.transpose(self.aux[0:NT, 0:P], g.negm, g.ident)\
                        .then_inc(self.mt_ready, 1)
            if main and n >= PV_LAG:
                self.pv_unit(nc, pe, s, n - PV_LAG)
                self.for_ends(n, PV_LAG + 1, lambda j: self.turn_chunk(nc, pe, s, j))
        if main:
            for n in range(NU - PV_LAG, NU):
                self.pv_unit(nc, pe, s, n)
            self.turn_chunk(nc, pe, s, NC - 1)

    def turn_chunk(self, nc, pe, s, j):
        R = self.D + 2
        pe.wait_ge(self.ot_taken, s * NC + j + 3)
        pe.wait_ge(self.norm_done, s * NC + j + 2)
        for ql in range(TPC):
            mm = nc.tensor.matmul(self.tr[:, ql, :], self.g.ot[0:R, j % 2, ql * P:(ql + 1) * P],
                                  self.g.ident[0:R, 0:R], is_transpose=R > 64, start=True, stop=True)
        mm.then_inc(self.tr_ready, 1)

    def pv_unit(self, nc, pe, s, n):
        g, b, D = self.g, self.parity(s), self.D
        j, kt = UNITS[n]
        if n == 0:
            self.wait_values(pe, s)
        if kt == 0:
            pe.wait_ge(self.ot_taken, s * NC + j + 1)
        pe.wait_ge(self.exp_done, s * NU + n + 3)
        off = max(0, kt - TPC * j) * P
        nc.tensor.matmul(self.pv[j % 2][0:D + 2, off:C], self.v[b][:, kt, :], g.pb[:, n % NPB, off:C],
                         start=kt == 0, stop=n == LAST_UNIT[j], skip_group_check=True)\
            .then_inc(self.pv_done, 1)

    def parity(self, s):
        return self.par

    def run(self, eng, step):
        self.par = 1
        step(-1, False, True)
        with eng.Fori(0, H // 2 - 1) as u:
            for self.par in range(2):
                step(u * 2 + self.par, True, True)
        self.par = 0
        step(H - 2, True, True)
        self.par = 1
        step(H - 1, True, False)


class AttentionA(Attention):
    D = DA
    KM = len(PAIRS) * DA
    KB = KM + PARTS
    ROWS = 16 * PARTS
    STAGE = 16 * 2 * len(PAIRS)

    def __init__(self, name, sem, g, arena):
        super().__init__(name, sem, g)
        self.tables = arena.f32(2, T)
        self.split = [arena.bf16(PARTS, T) for _ in range(2)]
        self.stack = [[arena.bf16(T) for _ in range(2)] for _ in range(2)]
        self.vall = arena.f32(NT, E)
        self.att = arena.f32(NT, E)
        vb = arena.f32(2, NT, DA + 2)
        self.v = [vb[:, i, :, :] for i in range(2)]
        self.tmp = arena.f32(2, 3, C)
        self.res = arena.f32(2, 2, C)
        self.mrow = arena.f32(3, P)
        self.mparts = arena.bf16(PARTS, P)
        B = g.bank
        self.st, self.sm, self.pv, self.aux = B[0:2], B[2:4], B[4:6], B[6]
        self.tr = B[7][:, 0:TPC * (DA + 2)].rearrange("p (t d) -> p t d", d=DA + 2)
        q, k = self.stack
        self.q_main, self.k_main = [a[0:self.KB] for a in q], [a[0:self.KB] for a in k]
        self.q_max, self.k_max = [a[0:self.KM] for a in q], [a[0:self.KM] for a in k]
        self.tables_in = sem(f"{name}_tables_in")
        self.proj_ready = sem(f"{name}_proj_ready")
        self.rope_done = sem(f"{name}_rope_done")
        self.vproj_ready = sem(f"{name}_vproj_ready")
        self.vproj_taken = sem(f"{name}_vproj_taken")
        self.staged = sem(f"{name}_staged")
        self.spilled = sem(f"{name}_spilled")
        self.v_ready = sem(f"{name}_v_ready")
        self.rope_own = sem(f"{name}_rope_own")
        self.row_own = sem(f"{name}_row_own")

    def tensor_project(self, nc, pe, ln):
        g = self.g
        n = 0
        pe.wait_ge(ln.xT_ready, NC)
        for which in range(2):
            for c in range(NC):
                if n >= 2:
                    pe.wait_ge(self.rope_done, n - 1)
                for turned in range(2):
                    mm = nc.tensor.matmul(g.bank[2 * (n % 2) + turned][:, :],
                                          g.wa[:, 2 * which + turned, :], g.xnT[:, c * C:(c + 1) * C],
                                          start=True, stop=True)
                mm.then_inc(self.proj_ready, 1)
                n += 1
        for c in range(NC):
            if c >= 2:
                pe.wait_ge(self.vproj_taken, c - 1)
            for t in range(TPC):
                mm = nc.tensor.matmul(g.bank[4 + c % 2][:, t * E:(t + 1) * E],
                                      g.xnT[:, (c * TPC + t) * P:(c * TPC + t + 1) * P],
                                      g.wa[:, 4, :], start=True, stop=True)
            mm.then_inc(self.vproj_ready, 1)

    def vector_project(self, nc, dve):
        g, chain = self.g, Chain(dve, self.rope_own)
        for i in range(2):
            chain.link(nc.vector.memset(self.stack[1][i][32:self.KB, :], 1.0))
            chain.link(nc.vector.memset(self.v[i], 1.0))
        nc.vector.memset(g.mpart, LOWEST).then_inc(self.consts, 1)
        dve.wait_ge(self.consts, 1)
        dve.wait_ge(self.tables_in, 32)
        n = 0
        for which in range(2):
            for c in range(NC):
                cols = slice(c * C, (c + 1) * C)
                tmp, res = self.tmp[:, n % 2], self.res[:, n % 2]
                dve.wait_ge(self.proj_ready, n + 1)
                for turned in range(2):
                    ins = nc.vector.scalar_tensor_tensor(
                        out=tmp[:, turned, :], in0=g.bank[2 * (n % 2) + turned][:, :],
                        scalar=g.ba[:, 2 * which + turned:2 * which + turned + 1],
                        in1=self.tables[:, turned, cols], op0=ALU.add, op1=ALU.mult)
                chain.link(ins)
                ins = nc.vector.tensor_tensor(tmp[:, 2, :], tmp[:, 0, :], tmp[:, 1, :], ALU.add)
                chain.link(ins)
                sp = self.split[which]
                chain.link(nc.vector.tensor_copy(sp[:, 0, cols], tmp[:, 2, :]))
                chain.link(nc.vector.tensor_tensor(res[:, 0, :], tmp[:, 2, :], sp[:, 0, cols], ALU.subtract))
                chain.link(nc.vector.tensor_copy(sp[:, 1, cols], res[:, 0, :]))
                chain.link(nc.vector.tensor_tensor(res[:, 1, :], res[:, 0, :], sp[:, 1, cols], ALU.subtract))
                nc.vector.tensor_copy(sp[:, 2, cols], res[:, 1, :]).then_inc(self.rope_done, 1)
                dve.wait_ge(self.rope_done, n + 1)
                n += 1
        for c in range(NC):
            dve.wait_ge(self.vproj_ready, c + 1)
            nc.vector.tensor_tensor(
                self.vall[:, c * TPC:(c + 1) * TPC, :],
                g.bank[4 + c % 2][:, :].rearrange("p (t e) -> p t e", e=E),
                g.bv.unsqueeze(1).to_broadcast([P, TPC, E]), ALU.add).then_inc(self.vproj_taken, 1)

    def sync_spill(self, sp):
        for which in range(2):
            sp.wait_ge(self.rope_done, NC * (which + 1))
            for part in range(PARTS):
                sp.dma_start(self.spill[which, part], self.split[which][:, part, :]).then_inc(self.spilled, 16)
        sp.wait_ge(self.spilled, 16 * 2 * PARTS)

    def sync_stage(self, sp, s):
        hp, b = s + 1, 1 - self.par
        for which in range(2):
            for r, pair in enumerate(PAIRS):
                sp.dma_start(self.stack[which][b][r * DA:(r + 1) * DA, :],
                             self.spill[which, pair[which], bass.ds(hp * DA, DA), :])\
                    .then_inc(self.staged, 16)

    def sync_step(self, nc, sp, s, main, prep):
        if not prep:
            return
        hp = s + 1
        if main:
            sp.wait_ge(self.st_ready, s * NU + self.ST_CREDIT)
        self.sync_stage(sp, s)
        sp.wait_ge(self.mt_taken, hp + 2)
        b = 1 - self.par
        for r in range(PARTS):
            sp.dma_start(self.stack[0][b][self.KM + r:self.KM + r + 1, :].rearrange("p (t q) -> p t q", q=P),
                         self.mparts[0:NT, r, :]).then_inc(self.rows_in, 16)

    def scalar_prepare(self, nc, act, s, n):
        if n != 0:
            return
        hp, b = s + 1, 1 - self.par
        if isinstance(s, int) and s < 0:
            act.wait_ge(self.vproj_taken, NC)
            act.wait_ge(self.consts, 1)
        else:
            act.wait_ge(self.pv_done, s * NU + NPB)
        nc.scalar.activation(self.v[b][:, :, 0:DA], self.vall[:, :, bass.ds(hp * DA, DA)], ACT.Copy)\
            .then_inc(self.v_ready, 1)

    def tensor_prepare(self, nc, pe, s, n):
        pass

    def wait_operands(self, pe, hp):
        pe.wait_ge(self.staged, self.STAGE * (hp + 1))

    def wait_turn_bank(self, pe, hp):
        pass

    def wait_values(self, pe, s):
        pe.wait_ge(self.v_ready, s + 1)

    def take_rows(self, nc, dve, hp):
        m, mp = self.mrow[0:NT], self.mparts[0:NT]
        steps = [lambda: nc.vector.tensor_copy(m[:, 0, :], self.aux[0:NT, 0:P]),
                 lambda: nc.vector.tensor_copy(mp[:, 0, :], m[:, 0, :]),
                 lambda: nc.vector.tensor_tensor(m[:, 1, :], m[:, 0, :], mp[:, 0, :], ALU.subtract),
                 lambda: nc.vector.tensor_copy(mp[:, 1, :], m[:, 1, :]),
                 lambda: nc.vector.tensor_tensor(m[:, 2, :], m[:, 1, :], mp[:, 1, :], ALU.subtract)]
        for i, step in enumerate(steps):
            step().then_inc(self.row_own, 1)
            dve.wait_ge(self.row_own, hp * len(steps) + i + 1)
        nc.vector.tensor_copy(mp[:, 2, :], m[:, 2, :]).then_inc(self.mt_taken, 1)


class AttentionB(Attention):
    D = DB
    KM = DB
    KB = DB + 1
    ROWS = 16
    GROUPS = 3 * NC
    AT = list(range(8)) + [10, 14, 18, 22]

    def __init__(self, name, sem, g, arena):
        super().__init__(name, sem, g)
        self.att = arena.f32(NT, H * DB)
        self.latT = arena.f32(T)
        self.wh = arena.f32(2, 3, DB)
        vb = arena.f32(2, NT, DB + 2)
        self.v = [vb[:, i, :, :] for i in range(2)]
        self.mrow = arena.f32(P)
        self.reuse_from = arena.at
        q, k = ([arena.f32(T) for _ in range(2)] for _ in range(2))
        qb, kb = ([arena.bf16(T) for _ in range(2)] for _ in range(2))
        self.q, self.k = q, k
        B = g.bank
        self.st, self.sm, self.pv, self.aux = B[0:2], B[2:4], B[4:6], B[6]
        self.tr = B[7][:, 0:TPC * (DB + 2)].rearrange("p (t d) -> p t d", d=DB + 2)
        self.q_main, self.k_main = [a[0:self.KB] for a in q], [a[0:self.KB] for a in k]
        self.q_max, self.k_max = [a[0:self.KM] for a in qb], [a[0:self.KM] for a in kb]
        self.lat_ready = sem(f"{name}_lat_ready")
        self.lat_taken = sem(f"{name}_lat_taken")
        self.wh_in = sem(f"{name}_wh_in")
        self.proj_ready = sem(f"{name}_proj_ready")
        self.proj_taken = sem(f"{name}_proj_taken")

    def tensor_project(self, nc, pe, ln):
        g = self.g
        pe.wait_ge(ln.xT_ready, NC)
        for c in range(NC):
            if c >= 2:
                pe.wait_ge(self.lat_taken, c - 1)
            nc.tensor.matmul(g.bank[c % 2][:, :], g.wdown, g.xnT[:, c * C:(c + 1) * C],
                             start=True, stop=True).then_inc(self.lat_ready, 1)
        pe.wait_ge(self.lat_taken, NC)

    def scalar_project(self, nc, act):
        g = self.g
        for c in range(NC):
            act.wait_ge(self.lat_ready, c + 1)
            nc.scalar.activation(self.latT[:, c * C:(c + 1) * C], g.bank[c % 2][:, :], ACT.Copy)\
                .then_inc(self.lat_taken, 1)
        act.wait_ge(self.consts, 1)

    def vector_project(self, nc, dve):
        for i in range(2):
            nc.vector.memset(self.k[i][DB:DB + 1, :], 1.0)
            nc.vector.memset(self.v[i], 1.0)
        nc.vector.memset(self.g.mpart, LOWEST).then_inc(self.consts, 1)
        dve.wait_ge(self.consts, 1)

    def scalar_credits(self, nc):
        super().scalar_credits(nc)
        nc.scalar.sem_inc(self.proj_taken, 1)

    def sync_credits(self, nc):
        pass

    def sync_weights(self, sp, hp, b):
        g = self.g
        sp.dma_start(self.wh[:, b, 0, :], g.w_q[:, bass.ds(hp * DB, DB)]).then_inc(self.wh_in, 16)
        sp.dma_start(self.wh[:, b, 1, :], g.w_up[:, bass.ds(hp * DB, DB)]).then_inc(self.wh_in, 16)
        sp.dma_start(self.wh[:, b, 2, :], g.w_up[:, bass.ds(hp * DB + H * DB, DB)]).then_inc(self.wh_in, 16)

    def sync_step(self, nc, sp, s, main, prep):
        if not prep:
            return
        hp, b = s + 1, 1 - self.par
        if main:
            sp.wait_ge(self.st_ready, s * NU + self.ST_CREDIT)
        self.sync_weights(sp, hp, b)
        sp.wait_ge(self.mt_taken, hp + 2)
        sp.dma_start(self.q[b][DB:DB + 1, :].rearrange("p (t q) -> p t q", q=P),
                     self.mrow[0:NT, :]).then_inc(self.rows_in, 16)

    def tensor_prepare(self, nc, pe, s, n):
        if n not in self.AT:
            return
        g, hp, b = self.g, s + 1, 1 - self.par
        k = self.AT.index(n)
        which, c = divmod(k, NC)
        out = self.aux
        if k == 0:
            pe.wait_ge(self.wh_in, 48 * (hp + 1))
            pe.wait_ge(self.mt_taken, hp + 1)
        pe.wait_ge(self.proj_taken, hp * self.GROUPS + k + 1)
        if which < 2:
            mm = nc.tensor.matmul(out[0:DB, :], self.wh[:, b, which, :],
                                  (g.xnT, self.latT)[which][:, c * C:(c + 1) * C], start=True, stop=True)
        else:
            for t in range(TPC):
                mm = nc.tensor.matmul(out[:, t * DB:(t + 1) * DB],
                                      self.latT[:, (c * TPC + t) * P:(c * TPC + t + 1) * P],
                                      self.wh[:, b, 2, :], start=True, stop=True)
        mm.then_inc(self.proj_ready, 1)

    def scalar_prepare(self, nc, act, s, n):
        if n not in self.AT:
            return
        hp, b = s + 1, 1 - self.par
        k = self.AT.index(n)
        which, c = divmod(k, NC)
        bank = self.aux
        act.wait_ge(self.proj_ready, hp * self.GROUPS + k + 1)
        if which < 2:
            cols = slice(c * C, (c + 1) * C)
            nc.scalar.activation((self.q, self.k)[which][b][0:DB, cols], bank[0:DB, :], ACT.Copy)
            nc.scalar.activation((self.q_max, self.k_max)[which][b][:, cols], bank[0:DB, :], ACT.Copy)\
                .then_inc(self.proj_taken, 1)
        else:
            nc.scalar.activation(self.v[b][:, c * TPC:(c + 1) * TPC, 0:DB],
                                 bank[:, 0:TPC * DB].rearrange("p (t d) -> p t d", d=DB), ACT.Copy)\
                .then_inc(self.proj_taken, 1)

    def wait_operands(self, pe, hp):
        pe.wait_ge(self.proj_taken, hp * self.GROUPS + 2 * NC + 1)

    def wait_turn_bank(self, pe, hp):
        pe.wait_ge(self.proj_taken, (hp + 1) * self.GROUPS + 1)

    def wait_values(self, pe, s):
        pe.wait_ge(self.proj_taken, (s + 1) * self.GROUPS + 1)

    def take_rows(self, nc, dve, hp):
        nc.vector.tensor_copy(self.mrow[0:NT, :], self.aux[0:NT, 0:P]).then_inc(self.mt_taken, 1)


class OutProj:

    def __init__(self, name, sem, g, arena, KT, att, w, bias, done, done_at):
        self.g, self.KT, self.att, self.w, self.bias = g, KT, att, w, bias
        self.done, self.done_at = done, done_at
        self.rows = arena.f32(2, KT * P)
        self.cols = arena.f32(2, KT * P)
        self.staged = sem(f"{name}_staged")
        self.turned = sem(f"{name}_turned")
        self.taken = sem(f"{name}_taken")
        self.y_ready = sem(f"{name}_y_ready")
        self.added = sem(f"{name}_added")
        self.bias_own = sem(f"{name}_bias_own")
        B = g.bank
        self.tb = [B[0:2], B[2:4]]
        self.yb = B[4:6]

    def run(self, eng, first, second):
        first(0, 0)
        with eng.Fori(0, NT // 2 - 1) as u:
            first(u * 2 + 1, 1)
            second(u * 2, 0)
            first(u * 2 + 2, 0)
            second(u * 2 + 1, 1)
        first(NT - 1, 1)
        second(NT - 2, 0)
        second(NT - 1, 1)

    def scalar(self, nc, act):
        nc.scalar.sem_inc(self.staged, 1)
        act.wait_ge(self.done, self.done_at)

        def stage(t, b):
            act.wait_ge(self.turned, t + 1)
            nc.scalar.activation(self.rows[:, b, :], self.att[:, bass.ds(t, 1), :], ACT.Copy)\
                .then_inc(self.staged, 1)
        self.run(act, stage, lambda t, b: None)

    def tensor(self, nc, pe):
        nc.tensor.sem_inc(self.turned, 2)
        nc.tensor.sem_inc(self.y_ready, 2)

        def turn(t, b):
            pe.wait_ge(self.staged, t + 2)
            pe.wait_ge(self.taken, t + 1)
            for k in range(self.KT):
                mm = nc.tensor.transpose(self.tb[b][k // TPC][:, k % TPC * P:(k % TPC + 1) * P],
                                         self.rows[:, b, k * P:(k + 1) * P], self.g.ident)
            mm.then_inc(self.turned, 1)

        def product(t, b):
            pe.wait_ge(self.taken, t + 3)
            pe.wait_ge(self.added, t + 1)
            for k in range(self.KT):
                mm = nc.tensor.matmul(self.yb[b][:, 0:E], self.cols[:, b, k * P:(k + 1) * P],
                                      self.w[:, k, :], start=k == 0, stop=k == self.KT - 1)
            mm.then_inc(self.y_ready, 1)
        self.run(pe, turn, product)

    def vector(self, nc, dve):
        g = self.g
        nc.vector.sem_inc(self.taken, 2)
        nc.vector.sem_inc(self.added, 2)

        def take(t, b):
            dve.wait_ge(self.turned, t + 3)
            dve.wait_ge(self.y_ready, t + 1)
            halves = range(0, self.KT, TPC)
            for k in halves:
                w = min(self.KT - k, TPC) * P
                ins = nc.vector.tensor_copy(self.cols[:, b, k * P:k * P + w], self.tb[b][k // TPC][:, 0:w])
            ins.then_inc(self.taken, 1)

        def add(t, b):
            dve.wait_ge(self.y_ready, t + 3)
            if self.bias is not None:
                nc.vector.tensor_tensor(g.x[:, bass.ds(t, 1), :], g.x[:, bass.ds(t, 1), :],
                                        self.bias.unsqueeze(1), ALU.add).then_inc(self.bias_own, 1)
                dve.wait_ge(self.bias_own, t + 1)
            nc.vector.tensor_tensor(g.x[:, bass.ds(t, 1), :], self.yb[b][:, 0:E].unsqueeze(1),
                                    g.x[:, bass.ds(t, 1), :], ALU.add).then_inc(self.added, 1)
        self.run(dve, take, add)
        dve.wait_ge(self.added, NT + 2)


class TreeFFN:

    def __init__(self, name, sem, g, arena):
        self.g = g
        self.act = arena.f32(2, 2, C)
        self.msk = arena.f32(2, 2, C)
        self.dec = arena.bf16(2, C)
        B = g.bank
        self.lg = [B[0:2], B[2:4]]
        self.cnt = B[4:6]
        self.y, self.yt = B[6], B[7]
        self.yrow = arena.f32(C)
        self.lg_ready = sem(f"{name}_lg_ready")
        self.silu_done = sem(f"{name}_silu_done")
        self.dec_done = sem(f"{name}_dec_done")
        self.cnt_ready = sem(f"{name}_cnt_ready")
        self.mask_done = sem(f"{name}_mask_done")
        self.out_done = sem(f"{name}_out_done")
        self.y_taken = sem(f"{name}_y_taken")
        self.y_turned = sem(f"{name}_y_turned")
        self.added = sem(f"{name}_added")

    def tensor(self, nc, pe, ln):
        g = self.g
        nc.tensor.sem_inc(self.cnt_ready, 4)
        nc.tensor.sem_inc(self.out_done, 2)
        pe.wait_ge(ln.xT_ready, NC)
        with pe.Fori(0, NC) as c:
            for p in range(TREES + 2):
                if p < TREES:
                    G = c * TREES + p
                    pe.wait_ge(self.silu_done, G * 2 + 2)
                    pe.wait_ge(self.dec_done, G + 1)
                    for leaf in range(2):
                        nc.tensor.matmul(self.lg[p % 2][leaf][:, :], g.win[:, 2 * p + leaf, :],
                                         g.xnT[:, bass.ds(c * C, C)], start=True, stop=True)\
                            .then_inc(self.lg_ready, 1)
                if 1 <= p <= TREES:
                    G = c * TREES + p - 1
                    pe.wait_ge(self.dec_done, G + 3)
                    pe.wait_ge(self.mask_done, G * 2 + 4)
                    for leaf in range(2):
                        nc.tensor.matmul(self.cnt[leaf][:, :], g.anc[:, leaf, :],
                                         self.dec[:, (p - 1) % 2, :], start=True, stop=True)\
                            .then_inc(self.cnt_ready, 1)
                if p >= 2:
                    r = p - 2
                    G = c * TREES + r
                    pe.wait_ge(self.mask_done, G * 2 + 6)
                    for leaf in range(2):
                        mm = nc.tensor.matmul(self.y[:, :], g.wout[:, 2 * r + leaf, :],
                                              self.msk[:, r % 2, leaf, :], start=r == 0 and leaf == 0,
                                              stop=r == TREES - 1 and leaf == 1)
                    mm.then_inc(self.out_done, 1)
            pe.wait_ge(self.y_taken, c + 1)
            pe.wait_ge(self.added, c + 1)
            for t in range(TPC):
                mm = nc.tensor.transpose(self.yt[:, t * P:(t + 1) * P], self.yrow[:, t * P:(t + 1) * P],
                                         g.ident)
            mm.then_inc(self.y_turned, 1)

    def scalar(self, nc, act):
        g = self.g
        nc.scalar.sem_inc(self.silu_done, 4)
        with act.Fori(0, NC) as c:
            for p in range(TREES):
                G = c * TREES + p
                act.wait_ge(self.mask_done, G * 2 + 2)
                for leaf in range(2):
                    act.wait_ge(self.lg_ready, G * 2 + leaf + 1)
                    nc.scalar.activation(self.act[:, p % 2, leaf, :], self.lg[p % 2][leaf][:, :], ACT.Silu,
                                         bias=g.bin[:, 2 * p + leaf:2 * p + leaf + 1])\
                        .then_inc(self.silu_done, 1)
            act.wait_ge(self.out_done, c * TREES + TREES + 2)
            nc.scalar.activation(self.yrow, self.y[:, :], ACT.Copy).then_inc(self.y_taken, 1)

    def vector(self, nc, dve):
        g = self.g
        nc.vector.sem_inc(self.dec_done, 2)
        nc.vector.sem_inc(self.mask_done, 4)
        nc.vector.sem_inc(self.added, 1)
        with dve.Fori(0, NC) as c:
            for p in range(TREES + 1):
                if p < TREES:
                    G = c * TREES + p
                    dve.wait_ge(self.silu_done, G * 2 + 5)
                    dve.wait_ge(self.cnt_ready, G * 2 + 2)
                    nc.vector.tensor_scalar(self.dec[:, p % 2, :], self.lg[p % 2][0][:, :],
                                            g.bin[:, 2 * p:2 * p + 1], 0.0, ALU.add, ALU.is_gt)\
                        .then_inc(self.dec_done, 1)
                if p >= 1:
                    q = p - 1
                    G = c * TREES + q
                    dve.wait_ge(self.silu_done, G * 2 + 6)
                    dve.wait_ge(self.out_done, G + 1)
                    for leaf in range(2):
                        dve.wait_ge(self.cnt_ready, G * 2 + 5 + leaf)
                        nc.vector.scalar_tensor_tensor(
                            out=self.msk[:, q % 2, leaf, :], in0=self.cnt[leaf][:, :],
                            scalar=g.nright[:, leaf:leaf + 1], in1=self.act[:, q % 2, leaf, :],
                            op0=ALU.is_equal, op1=ALU.mult).then_inc(self.mask_done, 1)
            dve.wait_ge(self.y_turned, c + 1)
            nc.vector.tensor_tensor(g.x[:, bass.ds(c * TPC, TPC), :],
                                    self.yt[:, :].rearrange("p (t e) -> p t e", e=E),
                                    g.x[:, bass.ds(c * TPC, TPC), :], ALU.add).then_inc(self.added, 1)
        dve.wait_ge(self.added, NC + 1)


class Shared:
    pass


def hybrid_kernel(nc, t, out):
    with ExitStack() as ctx:
        def sb(name, shape, dt):
            return ctx.enter_context(nc.sbuf_tensor(name, shape, dt))

        def sem(name):
            return ctx.enter_context(nc.semaphore(name))

        g = Shared()
        g.bank = [ctx.enter_context(nc.psum_tensor(f"bank{i}", [P, C], F32)) for i in range(8)]
        g.w_q, g.w_up = t["w_q"], t["w_up"]

        x = sb("x", [P, NT, E], F32)
        xnT = sb("xnT", [P, T], F32)
        win = sb("win", [P, 2 * TREES, P], F32)
        wout = sb("wout", [P, 2 * TREES, E], F32)
        wob = sb("wob", [P, H * DB // P, E], F32)
        wa = sb("wa", [P, 5, E], F32)
        wdown = sb("wdown", [P, P], F32)
        wproj = sb("wproj", [P, 1, E], F32)
        ba = sb("ba", [P, 4], F32)
        bv = sb("bv", [P, E], F32)
        bproj = sb("bproj", [P, E], F32)
        bin_ = sb("bin", [P, 2 * TREES], F32)
        ident = sb("ident", [P, P], F32)
        identb = sb("identb", [P, P], BF16)
        masks = sb("masks", [P, 2, P], BF16)
        anc = sb("anc", [P, 2, P], BF16)
        nright = sb("nright", [P, 2], F32)
        stats = sb("stats", [P, NT, 6], F32)
        mv = sb("mv", [P, NT, 2], F32)
        ve = sb("ve", [P, NT], F32)
        std = sb("std", [P, NT], F32)
        rstd = sb("rstd", [P, NT], F32)
        mpart = sb("mpart", [P, NT, NC], F32)
        negm = sb("negm", [P, NT], F32)
        rcp = sb("rcp", [P, 2, TPC], F32)
        words = H * DB * NT + T + 2 * 3 * DB + 2 * NT * (DB + 2) + P + 4 * T + 2 * T
        arena_t = sb("arena", [P, words], F32)
        pb = sb("pb", [P, NPB, C], F32)
        ot = sb("ot", [P, 2, C], F32)
        g.ot = ot
        g.x, g.xnT, g.win, g.wout, g.wa, g.wdown = x, xnT, win, wout, wa, wdown[:, :]
        g.ba, g.bv, g.bin = ba, bv[:, :], bin_
        g.ident, g.identb, g.mask_kq, g.mask_qk = ident[:, :], identb[:, :], masks[:, 0, :], masks[:, 1, :]
        g.anc, g.nright, g.stats, g.mv = anc, nright, stats, mv
        g.ve, g.std, g.rstd = ve[:, :], std[:, :], rstd[:, :]
        g.mpart, g.negm, g.rcp, g.pb = mpart[:, :, :], negm[:, :], rcp, pb

        g.x_in = sem("x_in")
        g.w_in = sem("w_in")
        g.stored = sem("stored")
        loads = [(ident[:, :], t["ident"]), (wa[:, :, :], t["wa"]), (ba[:, :], t["ba"]), (bv[:, :], t["bv"]),
                 (identb[:, :], t["identb"]), (masks[:, :, :], t["masks"]),
                 (wproj[:, 0, :], t["wproj"]), (bproj[:, :], t["bproj"]),
                 (win[:, :, :], t["win"]), (wout[:, :, :], t["wout"]), (bin_[:, :], t["bin"]),
                 (anc[:, :, :], t["anc"]), (nright[:, :], t["nright"]),
                 (wdown[:, :], t["w_down"]), (wob[:, :, :], t["w_out"])]
        g.W_ALL = 16 * len(loads)

        spill = nc.dram_tensor("qk_parts", (2, PARTS, E, T), BF16, kind="Internal").ap()

        def arena():
            return Arena(arena_t)

        ln = [Norm(f"ln{i}", sem, g) for i in range(4)]
        area = arena()
        att_a = AttentionA("a", sem, g, area)
        att_a.spill = spill
        proj_a = OutProj("pa", sem, g, area, 1, att_a.att, wproj, bproj[:, :],
                         att_a.norm_done, H * NC + 2)
        ffn_area = arena()
        ffn = []
        for i in range(2):
            ffn_area.at = area.at if i == 0 else 0
            ffn.append(TreeFFN(f"f{i}", sem, g, ffn_area))
        area = arena()
        att_b = AttentionB("b", sem, g, area)
        area.at = att_b.reuse_from
        proj_b = OutProj("pb", sem, g, area, H * DB // P, att_b.att, wob, None,
                         att_b.norm_done, H * NC + 2)
        xn = sb("xn", [P, 2, C], F32)
        g.xn = xn

        block = ctx.enter_context(nc.Block())

        @block.sync
        def _(sp):
            sp.dma_start(x[:, :, :], t["x"][0].rearrange("(t p) e -> p t e", p=P)).then_inc(g.x_in, 16)
            for dst, src in loads:
                sp.dma_start(dst, src).then_inc(g.w_in, 16)
            sp.dma_start(att_a.tables[:, 0, :], t["cos"]).then_inc(att_a.tables_in, 16)
            sp.dma_start(att_a.tables[:, 1, :], t["sin"]).then_inc(att_a.tables_in, 16)
            sp.sem_inc(att_a.rows_in, att_a.ROWS)
            att_a.sync_spill(sp)
            sp.wait_ge(att_a.consts, 1)
            att_a.run(sp, lambda *a: att_a.sync_step(nc, sp, *a))
            sp.sem_inc(att_b.rows_in, att_b.ROWS)
            sp.wait_ge(att_b.consts, 1)
            att_b.run(sp, lambda *a: att_b.sync_step(nc, sp, *a))
            sp.wait_ge(ffn[1].added, NC + 1)
            sp.dma_start(out[0].rearrange("(t p) e -> p t e", p=P), x[:, :, :]).then_inc(g.stored, 16)
            sp.wait_ge(g.stored, 16)

        @block.vector
        def _(dve):
            dve.wait_ge(g.x_in, 16)
            ln[0].vector(nc, dve)
            dve.wait_ge(g.w_in, g.W_ALL)
            att_a.vector_credits(nc)
            att_a.vector_project(nc, dve)
            att_a.run(dve, lambda *a: att_a.vector_step(nc, dve, *a))
            proj_a.vector(nc, dve)
            ln[1].vector(nc, dve)
            ffn[0].vector(nc, dve)
            ln[2].vector(nc, dve)
            att_b.vector_credits(nc)
            att_b.vector_project(nc, dve)
            att_b.run(dve, lambda *a: att_b.vector_step(nc, dve, *a))
            proj_b.vector(nc, dve)
            ln[3].vector(nc, dve)
            ffn[1].vector(nc, dve)

        @block.scalar
        def _(act):
            ln[0].scalar(nc, act)
            att_a.scalar_credits(nc)
            att_a.run(act, lambda *a: att_a.scalar_step(nc, act, *a))
            proj_a.scalar(nc, act)
            ln[1].scalar(nc, act)
            ffn[0].scalar(nc, act)
            ln[2].scalar(nc, act)
            att_b.scalar_credits(nc)
            att_b.scalar_project(nc, act)
            att_b.run(act, lambda *a: att_b.scalar_step(nc, act, *a))
            proj_b.scalar(nc, act)
            ln[3].scalar(nc, act)
            ffn[1].scalar(nc, act)

        @block.tensor
        def _(pe):
            pe.wait_ge(g.w_in, g.W_ALL)
            ln[0].tensor(nc, pe)
            att_a.tensor_credits(nc)
            att_a.tensor_project(nc, pe, ln[0])
            att_a.run(pe, lambda *a: att_a.tensor_step(nc, pe, *a))
            proj_a.tensor(nc, pe)
            ln[1].tensor(nc, pe)
            ffn[0].tensor(nc, pe, ln[1])
            ln[2].tensor(nc, pe)
            att_b.tensor_credits(nc)
            att_b.tensor_project(nc, pe, ln[2])
            att_b.run(pe, lambda *a: att_b.tensor_step(nc, pe, *a))
            proj_b.tensor(nc, pe)
            ln[3].tensor(nc, pe)
            ffn[1].tensor(nc, pe, ln[3])


def rope_tables(np):
    pos = np.arange(T, dtype=np.float32)
    inv = (1.0 / np.float32(10000.0) ** (np.arange(0, DA, 2, dtype=np.float32) / np.float32(DA))).astype(np.float32)
    freqs = inv[:, None] * pos[None, :]
    cos = np.repeat(np.cos(freqs), 2, axis=0)
    sin = np.repeat(np.sin(freqs), 2, axis=0) * np.tile(np.array([-1.0, 1.0], np.float32), DA // 2)[:, None]
    return (np.ascontiguousarray(np.tile(a, (H, 1)).astype(np.float32)) for a in (cos, sin))


def tree_tables(np):
    inner = 2 ** DEPTH - 1
    anc = np.zeros((P, 2, P), np.float32)
    right = np.zeros((P, 2), np.float32)
    for node in range(2 * inner + 1):
        leaf, col = (0, node) if node < inner else (1, node - inner)
        at = node
        while at > 0:
            up, step = (at - 1) // 2, 1 if at % 2 == 0 else -1
            anc[up, leaf, col] = step
            right[col, leaf] += step == 1
            at = up
    return anc, right


def kernel(**inputs):
    import numpy as np
    import ml_dtypes
    import concourse.bacc as bacc
    from concourse.bass_utils import run_bass_kernel_spmd as run

    a = {k: np.asarray(v) for k, v in inputs.items()}
    inner, nodes = 2 ** DEPTH - 1, 2 ** (DEPTH + 1) - 1
    bf16 = ml_dtypes.bfloat16
    cos, sin = rope_tables(np)
    anc, right = tree_tables(np)
    turned = np.arange(E) ^ 1
    W, b = a["L0_attn_a_Wqkv"], a["L0_attn_a_bqkv"]
    wq, wk, wv = W[:, :E], W[:, E:2 * E], W[:, 2 * E:]
    bq, bk, bv = b[:E], b[E:2 * E], b[2 * E:]

    def by_tree(w):
        w = w.reshape(TREES, nodes, *w.shape[1:])
        full = np.zeros((P, TREES, 2) + w.shape[2:], w.dtype)
        full[:inner, :, 0] = np.swapaxes(w[:, :inner], 0, 1)
        full[:, :, 1] = np.swapaxes(w[:, inner:], 0, 1)
        return full.reshape((P, 2 * TREES) + w.shape[2:])

    rows = np.arange(P)
    masks = np.zeros((P, 2, P), np.float32)
    masks[:, 0][rows[:, None] > rows[None, :]] = NEG
    masks[:, 1][rows[None, :] > rows[:, None]] = NEG
    arrays = {
        "x": a["L0_attn_a_x"],
        "wa": np.stack([wq, wq[:, turned], wk, wk[:, turned], wv], axis=1),
        "ba": np.stack([bq, bq[turned], bk, bk[turned]], axis=1),
        "bv": np.broadcast_to(bv, (P, E)),
        "wproj": a["L0_attn_a_Wproj"],
        "bproj": np.broadcast_to(a["L0_attn_a_bproj"], (P, E)),
        "w_down": a["L0_attn_b_w_kv_down"],
        "w_up": a["L0_attn_b_w_kv_up"],
        "w_q": a["L0_attn_b_w_q"],
        "w_out": a["L0_attn_b_w_out"].reshape(H * DB // P, P, E).transpose(1, 0, 2),
        "win": by_tree(a["L0_ffn_W_in"]).transpose(2, 1, 0),
        "bin": by_tree(a["L0_ffn_b_in"]),
        "wout": by_tree(a["L0_ffn_W_out"].T),
        "ident": np.eye(P, dtype=np.float32),
        "identb": np.eye(P, dtype=np.float32).astype(bf16),
        "masks": masks.astype(bf16),
        "anc": anc.astype(bf16),
        "nright": right,
        "cos": cos,
        "sin": sin,
    }
    nc = bacc.Bacc("TRN2", target_bir_lowering=False, num_devices=1)
    arrays = {k: np.ascontiguousarray(v) for k, v in arrays.items()}
    aps = {k: nc.dram_tensor(f"in_{k}", v.shape, mybir.dt.from_np(v.dtype), kind="ExternalInput").ap()
           for k, v in arrays.items()}
    out = nc.dram_tensor("out", (1, T, E), F32, kind="ExternalOutput").ap()
    hybrid_kernel(nc, aps, out)
    r = run(nc, [{f"in_{k}": v for k, v in arrays.items()}], core_ids=[0])
    return r.results[0]["out"]
```

```python
from contextlib import ExitStack

import concourse.bass as bass
from concourse import mybir

F32 = mybir.dt.float32
F32R = mybir.dt.float32r
BF16 = mybir.dt.bfloat16
ALU = mybir.AluOpType
ACT = mybir.ActivationFunctionType
AX = mybir.AxisListType

P = 128
T = 2048
E = 128
NT = T // P
C = 512
NC = T // C
TPC = C // P
H = 16
DA = E // H
DB = 64
EPS = 1e-5
NEG = -1e30
LOWEST = -3e38
TREES = 8
DEPTH = 7
PARTS = 3

UNITS = [(j, kt) for j in range(NC) for kt in range(TPC * (j + 1))]
PIECES = [(i, ch) for i in range(NT) for ch in range(i // TPC + 1)]
NU = len(UNITS)
NP = len(PIECES)
LAST_UNIT = {j: max(n for n, u in enumerate(UNITS) if u[0] == j) for j in range(NC)}
FIRST_MAX, END_MAX = 8, 34
TURN = 35
V_AT = 6
LO_LAG = 2
PV_LAG = 4
NB = 5
assert NU % NB == 0 and NU % 2 == 0 and NC % 2 == 0


def pieces_at(n):
    span = END_MAX - FIRST_MAX
    if not FIRST_MAX <= n < END_MAX:
        return range(0)
    return range((n - FIRST_MAX) * NP // span, (n + 1 - FIRST_MAX) * NP // span)


PAIRS = [(0, 0), (0, 1), (0, 2), (1, 0), (1, 1), (2, 0)]


class Chain:

    def __init__(self, eng, sem):
        self.eng, self.sem, self.n = eng, sem, 0

    def link(self, ins):
        ins.then_inc(self.sem, 1)
        self.n += 1
        self.eng.wait_ge(self.sem, self.n)


class Norm:

    def __init__(self, name, sem, g):
        self.g = g
        self.var_ready = sem(f"{name}_var_ready")
        self.std_ready = sem(f"{name}_std_ready")
        self.rows_ready = sem(f"{name}_rows_ready")
        self.turned = sem(f"{name}_turned")
        self.xT_ready = sem(f"{name}_xT_ready")
        self.own = sem(f"{name}_own")

    def vector(self, nc, dve):
        g, chain = self.g, Chain(dve, self.own)
        for t in range(NT):
            last = nc.vector.bn_stats(g.stats[:, t, :], g.x[:, t, :])
        chain.link(last)
        for t in range(NT):
            last = nc.vector.bn_aggr(g.mv[:, t, :], g.stats[:, t, :])
        chain.link(last)
        nc.vector.tensor_scalar(g.ve, g.mv[:, :, 1], EPS, None, ALU.add).then_inc(self.var_ready, 1)
        dve.wait_ge(self.std_ready, 1)
        chain.link(nc.vector.reciprocal(g.rstd, g.std))
        for c in range(NC):
            if c >= 2:
                dve.wait_ge(self.turned, c - 1)
            for t in range(TPC):
                n = TPC * c + t
                last = nc.vector.tensor_scalar(g.xn[:, c % 2, t * P:(t + 1) * P], g.x[:, n, :],
                                               g.mv[:, n, 0:1], g.rstd[:, n:n + 1],
                                               ALU.subtract, ALU.mult)
            last.then_inc(self.rows_ready, 1)

    def scalar(self, nc, act):
        g = self.g
        act.wait_ge(self.var_ready, 1)
        nc.scalar.activation(g.std, g.ve, ACT.Sqrt).then_inc(self.std_ready, 1)
        for c in range(NC):
            act.wait_ge(self.turned, c + 1)
            nc.scalar.activation(g.xnT[:, c * C:(c + 1) * C], g.bank[c % 2][:, :], ACT.Copy)\
                .then_inc(self.xT_ready, 1)

    def tensor(self, nc, pe):
        g = self.g
        for c in range(NC):
            pe.wait_ge(self.rows_ready, c + 1)
            if c >= 2:
                pe.wait_ge(self.xT_ready, c - 1)
            for t in range(TPC):
                last = nc.tensor.transpose(g.bank[c % 2][:, t * P:(t + 1) * P],
                                           g.xn[:, c % 2, t * P:(t + 1) * P], g.ident)
            last.then_inc(self.turned, 1)


class Attention:

    ROWS = None
    ST_CREDIT = 1
    VM = 66

    def __init__(self, name, sem, g):
        self.g = g
        self.st_ready = sem(f"{name}_scores_ready")
        self.exp_done = sem(f"{name}_exp_done")
        self.hi_done = sem(f"{name}_hi_done")
        self.lo_dve = sem(f"{name}_lo_dve")
        self.lo_pool = sem(f"{name}_lo_pool")
        self.pv_done = sem(f"{name}_pv_done")
        self.ot_taken = sem(f"{name}_ot_taken")
        self.tr_ready = sem(f"{name}_tr_ready")
        self.norm_done = sem(f"{name}_norm_done")
        self.mx_ready = sem(f"{name}_mx_ready")
        self.mx_done = sem(f"{name}_mx_done")
        self.negm_ready = sem(f"{name}_negm_ready")
        self.mt_ready = sem(f"{name}_mt_ready")
        self.mt_taken = sem(f"{name}_mt_taken")
        self.rows_in = sem(f"{name}_rows_in")
        self.own = sem(f"{name}_own")
        self.row_own = sem(f"{name}_row_own")
        self.consts = sem(f"{name}_consts")
        B = g.bank
        self.st, self.sm, self.pv, self.aux = B[0:2], B[2:4], B[4:6], B[6]
        self.tr = B[7][:, 0:TPC * (self.D + 2)].rearrange("p (t d) -> p t d", d=self.D + 2)
        self.lo_units = {"dve": [n for n in self.SPLIT if n not in self.LO_ON_POOL],
                         "pool": [n for n in self.SPLIT if n in self.LO_ON_POOL]}

    def offset(self, n):
        j, kt = UNITS[n]
        return max(0, kt - TPC * j) * P

    def wait_hi(self, eng, s, n):
        eng.wait_ge(self.hi_done, s * len(self.SPLIT) + self.SPLIT.index(n) + 1)

    def wait_lo(self, eng, s, n):
        for who, done in (("dve", self.lo_dve), ("pool", self.lo_pool)):
            mine = self.lo_units[who]
            if n % NU in mine:
                at = mine.index(n % NU) + 1 - (len(mine) if n < 0 else 0)
                eng.wait_ge(done, s * len(mine) + at + NB)

    def hi_part(self, nc, act, s, n):
        g, off = self.g, self.offset(n)
        act.wait_ge(self.exp_done, s * NU + n + 3)
        act.wait_ge(self.pv_done, s * NU + n + 1)
        nc.scalar.activation(g.hi[:, n % NB, off:C], g.pb[:, n % NB, off:C], ACT.Copy)\
            .then_inc(self.hi_done, 1)

    def lo_part(self, nc, eng, s, n):
        g, off = self.g, self.offset(n)
        on_pool = n in self.lo_units["pool"]
        self.wait_hi(eng, s, n)
        where = nc.gpsimd if on_pool else nc.vector
        where.tensor_tensor(g.lo[:, n % NB, off:C], g.pb[:, n % NB, off:C],
                            g.hi[:, n % NB, off:C].bitcast(F32), ALU.subtract)\
            .then_inc(self.lo_pool if on_pool else self.lo_dve, 1)

    def pool_step(self, nc, pool, s, main, prep, before):
        if main:
            for n in self.lo_units["pool"]:
                self.lo_part(nc, pool, s, n)

    def vector_credits(self, nc):
        nc.vector.sem_inc(self.norm_done, 2)
        nc.vector.sem_inc(self.ot_taken, 2)
        nc.vector.sem_inc(self.mx_done, 2)
        nc.vector.sem_inc(self.mt_taken, 1)
        nc.vector.sem_inc(self.lo_dve, NB)
        nc.vector.sem_inc(self.lo_pool, NB)

    def vector_lo(self, nc, dve, s, n):
        if n in self.lo_units["dve"]:
            self.lo_part(nc, dve, s, n)

    def vector_step(self, nc, dve, s, main, prep, before):
        g, D, hp = self.g, self.D, s + 1
        for n in range(NU):
            if before and n < LO_LAG:
                self.vector_lo(nc, dve, s - 1, NU + n - LO_LAG)
            if main and n >= LO_LAG:
                self.vector_lo(nc, dve, s, n - LO_LAG)
            if prep:
                self.vector_prepare(nc, dve, s, n)
                for m in pieces_at(n):
                    i, ch = PIECES[m]
                    w = self.piece_width(m)
                    dve.wait_ge(self.mx_ready, hp * NP + m + 1)
                    nc.vector.tensor_reduce(g.mpart[:, i, ch:ch + 1], self.sm[m % 2][:, 0:w],
                                            axis=AX.X, op=ALU.max).then_inc(self.mx_done, 1)
                    if m == NP - 1:
                        dve.wait_ge(self.mx_done, hp * NP + NP + 2)
                        nc.vector.tensor_reduce(g.negm, g.mpart, axis=AX.X, op=ALU.max,
                                                negate=True).then_inc(self.negm_ready, 1)
                if n == TURN:
                    dve.wait_ge(self.mt_ready, hp + 1)
                    dve.wait_ge(self.rows_in, self.ROWS * (hp + 1))
                    self.take_rows(nc, dve, hp)
            self.for_ends(s, n, PV_LAG, main, before, lambda *a: self.take_chunk(nc, dve, *a))
            self.for_ends(s, n, PV_LAG + 2, main, before, lambda *a: self.normalise(nc, dve, *a))

    def vector_end(self, nc, dve):
        for n in range(NU - LO_LAG, NU):
            self.vector_lo(nc, dve, H - 1, n)
        self.take_chunk(nc, dve, H - 1, NC - 1)
        self.normalise(nc, dve, H - 1, NC - 1)

    def for_ends(self, s, n, lag, main, before, do):
        for j in range(NC):
            if main and n - lag == LAST_UNIT[j]:
                do(s, j)
            if before and n - lag + NU == LAST_UNIT[j]:
                do(s - 1, j)

    def take_chunk(self, nc, dve, s, j):
        dve.wait_ge(self.pv_done, s * NU + LAST_UNIT[j] + 1 + NB)
        dve.wait_ge(self.tr_ready, s * NC + j + 1)
        nc.vector.tensor_copy(self.g.ot[0:self.VM, j % 2, :], self.pv[j % 2][0:self.VM, :])\
            .then_inc(self.ot_taken, 1)

    def normalise(self, nc, dve, s, j):
        g, D = self.g, self.D
        dve.wait_ge(self.tr_ready, s * NC + j + 3)
        dve.wait_ge(self.norm_done, s * NC + j + 1)
        self.wait_att(dve, s, j)
        nc.vector.reciprocal(g.rcp[:, j % 2, :], self.tr[:, :, D]).then_inc(self.own, 1)
        dve.wait_ge(self.own, s * NC + j + 1)
        nc.vector.tensor_tensor(self.att_out(s, j), self.tr[:, :, 0:D],
                                g.rcp[:, j % 2, :].unsqueeze(2).to_broadcast([P, TPC, D]),
                                ALU.mult).then_inc(self.norm_done, 1)

    def scalar_credits(self, nc):
        nc.scalar.sem_inc(self.exp_done, 2)

    def scalar_step(self, nc, act, s, main, prep, before):
        g = self.g
        for n in range(NU):
            off = self.offset(n)
            if main:
                act.wait_ge(self.st_ready, s * NU + n + 1 + self.ST_CREDIT)
                if (n - NB) % NU in self.SPLIT:
                    self.wait_lo(act, s, n - NB)
                else:
                    act.wait_ge(self.pv_done, s * NU + n + 1)
                nc.scalar.activation(g.pb[:, n % NB, off:C], self.st[n % 2][:, off:C], ACT.Exp,
                                     scale=self.D ** -0.5).then_inc(self.exp_done, 1)
                if n - 1 in self.SPLIT:
                    self.hi_part(nc, act, s, n - 1)
            if before and n == 0:
                self.hi_last(nc, act, s - 1)
            if prep:
                self.scalar_prepare(nc, act, s, n)

    def hi_last(self, nc, act, s):
        if NU - 1 in self.SPLIT:
            self.hi_part(nc, act, s, NU - 1)

    def scalar_end(self, nc, act):
        self.hi_last(nc, act, H - 1)

    def tensor_credits(self, nc):
        nc.tensor.sem_inc(self.st_ready, self.ST_CREDIT)
        nc.tensor.sem_inc(self.pv_done, NB)
        nc.tensor.sem_inc(self.tr_ready, 2)

    def piece_width(self, m):
        i, ch = PIECES[m]
        return min(C, (i + 1) * P - ch * C)

    def tensor_step(self, nc, pe, s, main, prep, before):
        g, b, hp = self.g, self.par, s + 1
        for n, (j, kt) in enumerate(UNITS):
            if main:
                if n == 0:
                    pe.wait_ge(self.rows_in, self.ROWS * (s + 2))
                off = self.offset(n)
                pe.wait_ge(self.exp_done, s * NU + n + 1)
                out = self.st[n % 2]
                pairs = self.main_pairs[b]
                for i, (k, q) in enumerate(pairs):
                    mm = nc.tensor.matmul(out[:, off:C], k[:, kt * P:(kt + 1) * P],
                                          q[:, j * C + off:(j + 1) * C], start=i == 0,
                                          stop=i == len(pairs) - 1 and kt < TPC * j)
                if kt >= TPC * j:
                    mm = nc.tensor.matmul(out[:, off:off + P], g.identb, g.mask_kq,
                                          start=False, stop=True)
                mm.then_inc(self.st_ready, 1)
            if prep:
                self.tensor_prepare(nc, pe, s, n)
                for m in pieces_at(n):
                    if m == 0:
                        self.wait_operands(pe, hp)
                    i, ch = PIECES[m]
                    w = self.piece_width(m)
                    pe.wait_ge(self.mx_done, hp * NP + m + 1)
                    out = self.sm[m % 2]
                    last = ch == i // TPC
                    mm = nc.tensor.matmul(out[:, 0:w], self.q_max[1 - b][:, i * P:(i + 1) * P],
                                          self.k_max[1 - b][:, ch * C:ch * C + w],
                                          start=True, stop=not last)
                    if last:
                        mm = nc.tensor.matmul(out[:, w - P:w], g.identb, g.mask_qk,
                                              start=False, stop=True)
                    mm.then_inc(self.mx_ready, 1)
                if n == TURN:
                    pe.wait_ge(self.negm_ready, hp + 1)
                    pe.wait_ge(self.mt_taken, hp + 1)
                    self.wait_turn_bank(pe, hp)
                    nc.tensor.transpose(self.aux[0:NT, 0:P], g.negm, g.ident)\
                        .then_inc(self.mt_ready, 1)
            if before and n < PV_LAG:
                self.pv_unit(nc, pe, s - 1, NU + n - PV_LAG, 1 - b)
            if main and n >= PV_LAG:
                self.pv_unit(nc, pe, s, n - PV_LAG, b)
            self.for_ends(s, n, PV_LAG + 1, main, before, lambda *a: self.turn_chunk(nc, pe, *a))

    def tensor_end(self, nc, pe):
        for n in range(NU - PV_LAG, NU):
            self.pv_unit(nc, pe, H - 1, n, 1)
        self.turn_chunk(nc, pe, H - 1, NC - 1)

    def turn_chunk(self, nc, pe, s, j):
        pe.wait_ge(self.ot_taken, s * NC + j + 3)
        pe.wait_ge(self.norm_done, s * NC + j + 2)
        for ql in range(TPC):
            ot = self.g.ot[0:self.VM, j % 2, ql * P:(ql + 1) * P]
            mm = nc.tensor.matmul(self.tr[:, ql, :], ot, self.merge, is_transpose=self.TURN_ONLY,
                                  start=True, stop=True)
        mm.then_inc(self.tr_ready, 1)

    def pv_unit(self, nc, pe, s, n, b):
        g, VM = self.g, self.VM
        j, kt = UNITS[n]
        if n == 0:
            self.wait_values(pe, s)
        if kt == 0:
            pe.wait_ge(self.ot_taken, s * NC + j + 1)
        off = self.offset(n)
        if n in self.SPLIT:
            self.wait_lo(pe, s, n)
            prods = self.value_products(b, kt, g.hi[:, n % NB, off:C], g.lo[:, n % NB, off:C])
        else:
            pe.wait_ge(self.exp_done, s * NU + n + 3)
            prods = [(self.vf[b][:, kt, :], g.pb[:, n % NB, off:C])]
        for i, (v, e) in enumerate(prods):
            mm = nc.tensor.matmul(self.pv[j % 2][0:v.shape[1], off:C], v, e, start=kt == 0 and i == 0,
                                  stop=n == LAST_UNIT[j] and i == len(prods) - 1,
                                  skip_group_check=True)
        mm.then_inc(self.pv_done, 1)

    def run(self, eng, step):
        self.par = 1
        step(-1, False, True, False)
        self.par = 0
        step(0, True, True, False)
        with eng.Fori(0, H // 2 - 1) as u:
            self.par = 1
            step(u * 2 + 1, True, True, True)
            self.par = 0
            step(u * 2 + 2, True, True, True)
        self.par = 1
        step(H - 1, True, False, True)


class AttentionA(Attention):
    D = DA
    KM = len(PAIRS) * DA
    KB = KM + PARTS
    ROWS = 16 * PARTS
    STAGE = 16 * 2 * PARTS
    SPLIT = [n for n in range(NU) if n % 10 not in (1, 5, 8)]
    assert {n for n, (_, kt) in enumerate(UNITS) if kt == 0} <= set(SPLIT)
    LO_ON_POOL = [n for n in range(NU) if n % 10 not in (4, )]
    TURN_ONLY = False

    def __init__(self, name, sem, g, sb):
        super().__init__(name, sem, g)
        self.tables = sb("a_tables", [P, 2, T], F32)
        self.split = [sb(f"a_split{i}", [P, PARTS, T], BF16) for i in range(2)]
        self.stack = [[sb(f"a_stack{i}{j}", [P, T], BF16) for j in range(2)] for i in range(2)]
        self.vall = sb("a_vall", [P, NT, H, 2, DA], F32R)
        self.att = sb("a_att", [P, NT, E], F32)
        self.v = [sb(f"a_v{i}", [P, NT, self.VM], F32R) for i in range(2)]
        self.vwhole = sb("a_vwhole", [P, NT, E], F32)
        self.vf = [sb(f"a_vf{i}", [P, NT, 2 * DA + 2], F32) for i in range(2)]
        self.tmp = sb("a_tmp", [P, 2, 3, C], F32)
        self.res = sb("a_res", [P, 2, 2, C], F32)
        self.mrow = sb("a_mrow", [P, 3, P], F32)
        self.mparts = sb("a_mparts", [P, PARTS, P], BF16)
        self.merge = g.merge_a
        q, k = self.stack
        self.main_pairs = [[(k[i][0:self.KB], q[i][0:self.KB])] for i in range(2)]
        self.q_max, self.k_max = [a[0:self.KM] for a in q], [a[0:self.KM] for a in k]
        self.tables_in = sem(f"{name}_tables_in")
        self.proj_ready = sem(f"{name}_proj_ready")
        self.rope_done = sem(f"{name}_rope_done")
        self.vproj_ready = sem(f"{name}_vproj_ready")
        self.vproj_taken = sem(f"{name}_vproj_taken")
        self.staged = sem(f"{name}_staged")
        self.spilled = sem(f"{name}_spilled")
        self.v_ready = sem(f"{name}_v_ready")
        self.rope_own = sem(f"{name}_rope_own")

    def att_out(self, s, j):
        return self.att[:, TPC * j:TPC * (j + 1), bass.ds(s * DA, DA)]

    def wait_att(self, dve, s, j):
        pass

    def value_products(self, b, kt, hi, lo):
        v = self.v[b][:, kt, :]
        return [(v, hi), (v, lo)]

    def tensor_project(self, nc, pe, ln):
        g = self.g
        n = 0
        pe.wait_ge(ln.xT_ready, NC)
        for which in range(2):
            for c in range(NC):
                if n >= 2:
                    pe.wait_ge(self.rope_done, n - 1)
                for turned in range(2):
                    mm = nc.tensor.matmul(g.bank[2 * (n % 2) + turned][:, :],
                                          g.wa[:, 2 * which + turned, :], g.xnT[:, c * C:(c + 1) * C],
                                          start=True, stop=True)
                mm.then_inc(self.proj_ready, 1)
                n += 1
        for c in range(NC):
            if c >= 2:
                pe.wait_ge(self.vproj_taken, c - 1)
            for t in range(TPC):
                mm = nc.tensor.matmul(g.bank[4 + c % 2][:, t * E:(t + 1) * E],
                                      g.xnT[:, (c * TPC + t) * P:(c * TPC + t + 1) * P],
                                      g.wa[:, 4, :], start=True, stop=True)
            mm.then_inc(self.vproj_ready, 1)

    def vector_project(self, nc, dve):
        g, chain = self.g, Chain(dve, self.rope_own)
        for i in range(2):
            chain.link(nc.vector.memset(self.stack[1][i][32:self.KB, :], 1.0))
            chain.link(nc.vector.memset(self.v[i][:, :, :].bitcast(F32), 0.0))
            chain.link(nc.vector.memset(self.v[i][:, :, 2 * DA:2 * DA + 1].bitcast(F32), 1.0))
            chain.link(nc.vector.memset(self.vf[i][:, :, :], 0.0))
            chain.link(nc.vector.memset(self.vf[i][:, :, 2 * DA:2 * DA + 1], 1.0))
        nc.vector.memset(g.mpart, LOWEST).then_inc(self.consts, 1)
        dve.wait_ge(self.consts, 1)
        dve.wait_ge(self.tables_in, 32)
        n = 0
        for which in range(2):
            for c in range(NC):
                cols = slice(c * C, (c + 1) * C)
                tmp, res = self.tmp[:, n % 2], self.res[:, n % 2]
                dve.wait_ge(self.proj_ready, n + 1)
                for turned in range(2):
                    ins = nc.vector.scalar_tensor_tensor(
                        out=tmp[:, turned, :], in0=g.bank[2 * (n % 2) + turned][:, :],
                        scalar=g.ba[:, 2 * which + turned:2 * which + turned + 1],
                        in1=self.tables[:, turned, cols], op0=ALU.add, op1=ALU.mult)
                chain.link(ins)
                chain.link(nc.vector.tensor_tensor(tmp[:, 2, :], tmp[:, 0, :], tmp[:, 1, :], ALU.add))
                sp = self.split[which]
                chain.link(nc.vector.tensor_copy(sp[:, 0, cols], tmp[:, 2, :]))
                chain.link(nc.vector.tensor_tensor(res[:, 0, :], tmp[:, 2, :], sp[:, 0, cols], ALU.subtract))
                chain.link(nc.vector.tensor_copy(sp[:, 1, cols], res[:, 0, :]))
                chain.link(nc.vector.tensor_tensor(res[:, 1, :], res[:, 0, :], sp[:, 1, cols], ALU.subtract))
                nc.vector.tensor_copy(sp[:, 2, cols], res[:, 1, :]).then_inc(self.rope_done, 1)
                dve.wait_ge(self.rope_done, n + 1)
                n += 1
        for c in range(NC):
            dve.wait_ge(self.vproj_ready, c + 1)
            tiles = slice(c * TPC, (c + 1) * TPC)
            rows = self.vwhole[:, tiles, :].rearrange("p t (h d) -> p t h d", h=H, d=DA)
            chain.link(nc.vector.tensor_tensor(
                self.vwhole[:, tiles, :],
                g.bank[4 + c % 2][:, :].rearrange("p (t e) -> p t e", e=E),
                g.bv.unsqueeze(1).to_broadcast([P, TPC, E]), ALU.add))
            hi, lo = self.vall[:, tiles, :, 0, :], self.vall[:, tiles, :, 1, :]
            chain.link(nc.vector.tensor_copy(hi, rows))
            nc.vector.tensor_tensor(lo, rows, hi.bitcast(F32), ALU.subtract).then_inc(self.vproj_taken, 1)

    def vector_prepare(self, nc, dve, s, n):
        pass

    def sync_spill(self, sp):
        for which in range(2):
            sp.wait_ge(self.rope_done, NC * (which + 1))
            for part in range(PARTS):
                sp.dma_start(self.g.spill[which, part], self.split[which][:, part, :])\
                    .then_inc(self.spilled, 16)
        sp.wait_ge(self.spilled, 16 * 2 * PARTS)

    def sync_step(self, nc, sp, s, main, prep, before):
        if not prep:
            return
        hp, b = s + 1, 1 - self.par
        if main:
            sp.wait_ge(self.st_ready, s * NU + self.ST_CREDIT)
        at = 0
        for part in range(PARTS):
            R = PARTS - part
            rows = slice(at * DA, (at + R) * DA)
            sp.dma_start(self.stack[1][b][rows, :], self.g.spill[1, 0:R, bass.ds(hp * DA, DA), :])\
                .then_inc(self.staged, 16)
            sp.dma_start(self.stack[0][b][rows, :],
                         self.g.spill[0, part:part + 1, bass.ds(hp * DA, DA), :].to_broadcast([R, DA, T]))\
                .then_inc(self.staged, 16)
            at += R
        sp.wait_ge(self.mt_taken, hp + 2)
        for r in range(PARTS):
            sp.dma_start(self.stack[0][b][self.KM + r:self.KM + r + 1, :].rearrange("p (t q) -> p t q", q=P),
                         self.mparts[0:NT, r, :]).then_inc(self.rows_in, 16)

    def scalar_prepare(self, nc, act, s, n):
        if n != V_AT:
            return
        hp, b = s + 1, 1 - self.par
        if isinstance(s, int) and s < 0:
            act.wait_ge(self.vproj_taken, NC)
            act.wait_ge(self.consts, 1)
        else:
            act.wait_ge(self.pv_done, s * NU + NB)
        nc.scalar.activation(self.vf[b][:, :, 0:DA], self.vwhole[:, :, bass.ds(hp * DA, DA)], ACT.Copy)
        nc.scalar.activation(
            self.v[b][:, :, 0:2 * DA],
            self.vall[:, :, :, :, :].rearrange("p t h c d -> p t (h c d)")
                [:, :, bass.ds(hp * 2 * DA, 2 * DA)].bitcast(F32), ACT.Copy).then_inc(self.v_ready, 1)

    def tensor_prepare(self, nc, pe, s, n):
        pass

    def wait_operands(self, pe, hp):
        pe.wait_ge(self.staged, self.STAGE * (hp + 1))

    def wait_turn_bank(self, pe, hp):
        pass

    def wait_values(self, pe, s):
        pe.wait_ge(self.v_ready, s + 1)

    def take_rows(self, nc, dve, hp):
        m, mp = self.mrow[0:NT], self.mparts[0:NT]
        steps = [lambda: nc.vector.tensor_copy(m[:, 0, :], self.aux[0:NT, 0:P]),
                 lambda: nc.vector.tensor_copy(mp[:, 0, :], m[:, 0, :]),
                 lambda: nc.vector.tensor_tensor(m[:, 1, :], m[:, 0, :], mp[:, 0, :], ALU.subtract),
                 lambda: nc.vector.tensor_copy(mp[:, 1, :], m[:, 1, :]),
                 lambda: nc.vector.tensor_tensor(m[:, 2, :], m[:, 1, :], mp[:, 1, :], ALU.subtract)]
        for i, step in enumerate(steps):
            step().then_inc(self.row_own, 1)
            dve.wait_ge(self.row_own, hp * len(steps) + i + 1)
        nc.vector.tensor_copy(mp[:, 2, :], m[:, 2, :]).then_inc(self.mt_taken, 1)


class AttentionB(Attention):
    D = DB
    ROWS = 16 * 2
    GROUPS = 3 * NC
    AT = list(range(8)) + [10, 14, 18, 22]
    SPLIT = list(range(NU))
    LO_ON_POOL = [n for n in range(NU) if n % 2 == 0]
    TURN_ONLY = True

    def __init__(self, name, sem, g, sb):
        super().__init__(name, sem, g)
        self.att = sb("b_att", [P, 2, TPC, DB], F32)
        self.latT = sb("b_latT", [P, T], F32)
        self.wh = sb("b_wh", [P, 2, 5, DB], F32)
        self.v1 = [sb(f"b_v1{i}", [P, NT, self.VM], F32R) for i in range(2)]
        self.v2 = [sb(f"b_v2{i}", [P, NT, self.VM], F32R) for i in range(2)]
        self.mrow = sb("b_mrow", [P, 2, P], F32R)
        self.q1, self.q2, self.k1, self.k2 = ([sb(f"b_{x}{i}", [P, T], F32R) for i in range(2)]
                                              for x in ("q1", "q2", "k1", "k2"))
        R = DB + 2
        self.merge = g.ident[0:R, 0:R]
        self.main_pairs = [[(self.k1[i][:, :], self.q1[i][:, :]),
                            (self.k2[i][0:R], self.q2[i][0:R])] for i in range(2)]
        self.q_max, self.k_max = self.q1, self.k1
        self.lat_ready = sem(f"{name}_lat_ready")
        self.lat_taken = sem(f"{name}_lat_taken")
        self.wh_in = sem(f"{name}_wh_in")
        self.proj_ready = sem(f"{name}_proj_ready")
        self.proj_hi = sem(f"{name}_proj_hi")
        self.proj_taken = sem(f"{name}_proj_taken")
        self.stored = [sem(f"{name}_stored{i}") for i in range(2)]

    def att_out(self, s, j):
        return self.att[:, j % 2, :, :]

    def wait_att(self, dve, s, j):
        dve.wait_ge(self.stored[j % 2], (s * (NC // 2) + j // 2 + 1) * 16)

    def value_products(self, b, kt, hi, lo):
        v1, v2 = self.v1[b][:, kt, :], self.v2[b][:, kt, :]
        return [(v1, hi), (v1, lo), (v2, hi)]

    def tensor_project(self, nc, pe, ln):
        g = self.g
        pe.wait_ge(ln.xT_ready, NC)
        for c in range(NC):
            if c >= 2:
                pe.wait_ge(self.lat_taken, c - 1)
            nc.tensor.matmul(g.bank[c % 2][:, :], g.wdown, g.xnT[:, c * C:(c + 1) * C],
                             start=True, stop=True).then_inc(self.lat_ready, 1)
        pe.wait_ge(self.lat_taken, NC)

    def scalar_project(self, nc, act):
        g = self.g
        for c in range(NC):
            act.wait_ge(self.lat_ready, c + 1)
            nc.scalar.activation(self.latT[:, c * C:(c + 1) * C], g.bank[c % 2][:, :], ACT.Copy)\
                .then_inc(self.lat_taken, 1)
        act.wait_ge(self.consts, 1)

    def vector_project(self, nc, dve):
        for i in range(2):
            nc.vector.memset(self.k2[i][DB:DB + 2, :].bitcast(F32), 1.0)
            nc.vector.memset(self.v1[i][:, :, DB:].bitcast(F32), 1.0)
            nc.vector.memset(self.v2[i][:, :, DB:].bitcast(F32), 0.0)
        nc.vector.memset(self.g.mpart, LOWEST).then_inc(self.consts, 1)
        dve.wait_ge(self.consts, 1)

    def vector_credits(self, nc):
        super().vector_credits(nc)
        nc.vector.sem_inc(self.proj_taken, 2)

    def group(self, n):
        k = self.AT.index(n)
        which, c = divmod(k, NC)
        return k, which, c, self.sm[k % 2] if which < 2 else self.aux

    def sync_step(self, nc, sp, s, main, prep, before):
        g = self.g
        hp, b = s + 1, 1 - self.par
        if prep:
            if main:
                sp.wait_ge(self.st_ready, s * NU + self.ST_CREDIT)
            for i, (w, at) in enumerate([(g.w_q, 0), (g.w_q, 0), (g.w_up, 0), (g.w_up, 0), (g.w_up, H * DB)]):
                sp.dma_start(self.wh[:, b, i, :], w[:, bass.ds(hp * DB + at, DB)]).then_inc(self.wh_in, 16)
        if before:
            self.store_chunk(sp, s - 1, NC - 1)
        for j in range(NC - 1):
            if main:
                self.store_chunk(sp, s, j)
            if j == NC - 2 and prep:
                sp.wait_ge(self.mt_taken, hp + 2)
                for r in range(2):
                    sp.dma_start(self.q2[b][DB + r:DB + r + 1, :].bitcast(F32)
                                     .rearrange("p (t q) -> p t q", q=P),
                                 self.mrow[0:NT, r, :].bitcast(F32)).then_inc(self.rows_in, 16)

    def store_chunk(self, sp, s, j):
        sp.wait_ge(self.norm_done, s * NC + j + 3)
        sp.dma_start(self.g.att_dram[:, TPC * j:TPC * (j + 1), bass.ds(s * DB, DB)],
                     self.att[:, j % 2, :, :]).then_inc(self.stored[j % 2], 16)

    def tensor_prepare(self, nc, pe, s, n):
        if n not in self.AT:
            return
        g, hp, b = self.g, s + 1, 1 - self.par
        k, which, c, out = self.group(n)
        if k == 0:
            pe.wait_ge(self.wh_in, 80 * (hp + 1))
            pe.wait_ge(self.mx_done, hp * NP + 2)
        if k == 2 * NC:
            pe.wait_ge(self.mt_taken, hp + 1)
        pe.wait_ge(self.proj_taken, hp * self.GROUPS + (k + 1 if which < 2 else k + 2))
        if which < 2:
            mm = nc.tensor.matmul(out[:, :],
                                  self.wh[:, b, 2 * which:2 * which + 2, :].rearrange("p a d -> p (a d)"),
                                  (g.xnT, self.latT)[which][:, c * C:(c + 1) * C], start=True, stop=True)
        else:
            for t in range(TPC):
                mm = nc.tensor.matmul(out[:, t * DB:(t + 1) * DB],
                                      self.latT[:, (c * TPC + t) * P:(c * TPC + t + 1) * P],
                                      self.wh[:, b, 4, :], start=True, stop=True)
        mm.then_inc(self.proj_ready, 1)

    def scalar_prepare(self, nc, act, s, n):
        if n not in self.AT:
            return
        hp, b = s + 1, 1 - self.par
        k, which, c, bank = self.group(n)
        cols = slice(c * C, (c + 1) * C)
        act.wait_ge(self.proj_ready, hp * self.GROUPS + k + 1)
        if which == 0:
            nc.scalar.activation(self.q1[b][:, cols], bank[:, :], ACT.Copy)
            ins = nc.scalar.activation(self.q2[b][0:DB, cols], bank[0:DB, :], ACT.Copy)
        elif which == 1:
            ins = nc.scalar.activation(self.k1[b][:, cols], bank[:, :], ACT.Copy)
        else:
            ins = nc.scalar.activation(self.v1[b][:, c * TPC:(c + 1) * TPC, 0:DB],
                                       bank[:, 0:TPC * DB].rearrange("p (t d) -> p t d", d=DB), ACT.Copy)
        ins.then_inc(self.proj_hi, 1)

    def vector_prepare(self, nc, dve, s, n):
        if n not in self.AT:
            return
        hp, b = s + 1, 1 - self.par
        k, which, c, bank = self.group(n)
        cols = slice(c * C, (c + 1) * C)
        dve.wait_ge(self.proj_hi, hp * self.GROUPS + k + 1)
        if which == 0:
            out, x, hi = self.q1[b][DB:P, cols], bank[DB:P, :], self.q1[b][DB:P, cols]
        elif which == 1:
            out, x, hi = self.k2[b][0:DB, cols], bank[0:DB, :], self.k1[b][0:DB, cols]
        else:
            tiles = slice(c * TPC, (c + 1) * TPC)
            out, hi = self.v2[b][:, tiles, 0:DB], self.v1[b][:, tiles, 0:DB]
            x = bank[:, 0:TPC * DB].rearrange("p (t d) -> p t d", d=DB)
        nc.vector.tensor_tensor(out, x, hi.bitcast(F32), ALU.subtract).then_inc(self.proj_taken, 1)

    def wait_operands(self, pe, hp):
        pe.wait_ge(self.proj_taken, hp * self.GROUPS + 2 * NC + 2)

    def wait_turn_bank(self, pe, hp):
        pe.wait_ge(self.proj_taken, (hp + 1) * self.GROUPS + 2)

    def wait_values(self, pe, s):
        pe.wait_ge(self.proj_taken, (s + 1) * self.GROUPS + 2)

    def take_rows(self, nc, dve, hp):
        m, mt = self.mrow[0:NT], self.aux[0:NT, 0:P]
        nc.vector.tensor_copy(m[:, 0, :], mt).then_inc(self.row_own, 1)
        dve.wait_ge(self.row_own, hp + 1)
        nc.vector.tensor_tensor(m[:, 1, :], mt, m[:, 0, :].bitcast(F32), ALU.subtract)\
            .then_inc(self.mt_taken, 1)


class OutProj:

    def __init__(self, name, sem, g, sb, KT, att, w, bias, done):
        self.g, self.KT, self.att, self.w, self.bias = g, KT, att, w, bias
        self.done = done
        self.rows = sb(f"{name}_rows", [P, 2, KT * P], F32)
        self.cols = sb(f"{name}_cols", [P, 2, KT * P], F32)
        self.staged = [sem(f"{name}_staged{i}") for i in range(2)]
        self.turned = sem(f"{name}_turned")
        self.taken = sem(f"{name}_taken")
        self.y_ready = sem(f"{name}_y_ready")
        self.added = sem(f"{name}_added")
        self.bias_own = sem(f"{name}_bias_own")
        B = g.bank
        self.tb = [B[0:2], B[2:4]]
        self.yb = B[4:6]

    def run(self, eng, first, second):
        first(0, 0, 0)
        with eng.Fori(0, NT // 2 - 1) as u:
            first(u * 2 + 1, 1, u)
            second(u * 2, 0)
            first(u * 2 + 2, 0, u + 1)
            second(u * 2 + 1, 1)
        first(NT - 1, 1, NT // 2 - 1)
        second(NT - 2, 0)
        second(NT - 1, 1)

    UNIT = 1

    def sync(self, sp):
        self.UNIT = 16
        for what, count in self.done:
            sp.wait_ge(what, count)

        def stage(t, b, half):
            sp.wait_ge(self.turned, t + 1)
            sp.dma_start(self.rows[:, b, :].unsqueeze(1), self.att[:, bass.ds(t, 1), :])\
                .then_inc(self.staged[b], 16)
        self.run(sp, stage, lambda t, b: None)

    def scalar(self, nc, act):
        for what, count in self.done:
            act.wait_ge(what, count)

        def stage(t, b, half):
            act.wait_ge(self.turned, t + 1)
            nc.scalar.activation(self.rows[:, b, :], self.att[:, bass.ds(t, 1), :], ACT.Copy)\
                .then_inc(self.staged[b], 1)
        self.run(act, stage, lambda t, b: None)

    def tensor(self, nc, pe):
        nc.tensor.sem_inc(self.turned, 2)
        nc.tensor.sem_inc(self.y_ready, 2)

        def turn(t, b, half):
            pe.wait_ge(self.staged[b], (half + 1) * self.UNIT)
            pe.wait_ge(self.taken, t + 1)
            for k in range(self.KT):
                mm = nc.tensor.transpose(self.tb[b][k // TPC][:, k % TPC * P:(k % TPC + 1) * P],
                                         self.rows[:, b, k * P:(k + 1) * P], self.g.ident)
            mm.then_inc(self.turned, 1)

        def product(t, b):
            pe.wait_ge(self.taken, t + 3)
            pe.wait_ge(self.added, t + 1)
            for k in range(self.KT):
                mm = nc.tensor.matmul(self.yb[b][:, 0:E], self.cols[:, b, k * P:(k + 1) * P],
                                      self.w[:, k, :], start=k == 0, stop=k == self.KT - 1)
            mm.then_inc(self.y_ready, 1)
        self.run(pe, turn, product)

    def vector(self, nc, dve):
        g = self.g
        nc.vector.sem_inc(self.taken, 2)
        nc.vector.sem_inc(self.added, 2)

        def take(t, b, half):
            dve.wait_ge(self.turned, t + 3)
            dve.wait_ge(self.y_ready, t + 1)
            halves = range(0, self.KT, TPC)
            for k in halves:
                w = min(self.KT - k, TPC) * P
                ins = nc.vector.tensor_copy(self.cols[:, b, k * P:k * P + w], self.tb[b][k // TPC][:, 0:w])
            ins.then_inc(self.taken, 1)

        def add(t, b):
            dve.wait_ge(self.y_ready, t + 3)
            if self.bias is not None:
                nc.vector.tensor_tensor(g.x[:, bass.ds(t, 1), :], g.x[:, bass.ds(t, 1), :],
                                        self.bias.unsqueeze(1), ALU.add).then_inc(self.bias_own, 1)
                dve.wait_ge(self.bias_own, t + 1)
            nc.vector.tensor_tensor(g.x[:, bass.ds(t, 1), :], self.yb[b][:, 0:E].unsqueeze(1),
                                    g.x[:, bass.ds(t, 1), :], ALU.add).then_inc(self.added, 1)
        self.run(dve, take, add)
        dve.wait_ge(self.added, NT + 2)


class TreeFFN:

    def __init__(self, name, sem, g, sb):
        self.g = g
        self.act = sb(f"{name}_act", [P, 2, 2, C], F32)
        self.msk = sb(f"{name}_msk", [P, 2, 2, C], F32)
        self.dec = sb(f"{name}_dec", [P, 2, C], BF16)
        B = g.bank
        self.lg = [B[0:2], B[2:4]]
        self.cnt = B[4:6]
        self.y, self.yt = B[6], B[7]
        self.yrow = sb(f"{name}_yrow", [P, C], F32)
        self.lg_ready = sem(f"{name}_lg_ready")
        self.silu_done = sem(f"{name}_silu_done")
        self.dec_done = sem(f"{name}_dec_done")
        self.cnt_ready = sem(f"{name}_cnt_ready")
        self.mask_done = sem(f"{name}_mask_done")
        self.out_done = sem(f"{name}_out_done")
        self.y_taken = sem(f"{name}_y_taken")
        self.y_turned = sem(f"{name}_y_turned")
        self.added = sem(f"{name}_added")

    def tensor(self, nc, pe, ln):
        g = self.g
        nc.tensor.sem_inc(self.cnt_ready, 4)
        nc.tensor.sem_inc(self.out_done, 2)
        pe.wait_ge(ln.xT_ready, NC)
        with pe.Fori(0, NC) as c:
            for p in range(TREES + 2):
                if p < TREES:
                    G = c * TREES + p
                    pe.wait_ge(self.silu_done, G * 2 + 2)
                    pe.wait_ge(self.dec_done, G + 1)
                    for leaf in range(2):
                        nc.tensor.matmul(self.lg[p % 2][leaf][:, :], g.win[:, 2 * p + leaf, :],
                                         g.xnT[:, bass.ds(c * C, C)], start=True, stop=True)\
                            .then_inc(self.lg_ready, 1)
                if 1 <= p <= TREES:
                    G = c * TREES + p - 1
                    pe.wait_ge(self.dec_done, G + 3)
                    pe.wait_ge(self.mask_done, G * 2 + 4)
                    for leaf in range(2):
                        nc.tensor.matmul(self.cnt[leaf][:, :], g.anc[:, leaf, :],
                                         self.dec[:, (p - 1) % 2, :], start=True, stop=True)\
                            .then_inc(self.cnt_ready, 1)
                if p >= 2:
                    r = p - 2
                    G = c * TREES + r
                    pe.wait_ge(self.mask_done, G * 2 + 6)
                    for leaf in range(2):
                        mm = nc.tensor.matmul(self.y[:, :], g.wout[:, 2 * r + leaf, :],
                                              self.msk[:, r % 2, leaf, :], start=r == 0 and leaf == 0,
                                              stop=r == TREES - 1 and leaf == 1)
                    mm.then_inc(self.out_done, 1)
            pe.wait_ge(self.y_taken, c + 1)
            pe.wait_ge(self.added, c + 1)
            for t in range(TPC):
                mm = nc.tensor.transpose(self.yt[:, t * P:(t + 1) * P], self.yrow[:, t * P:(t + 1) * P],
                                         g.ident)
            mm.then_inc(self.y_turned, 1)

    def scalar(self, nc, act):
        g = self.g
        nc.scalar.sem_inc(self.silu_done, 4)
        with act.Fori(0, NC) as c:
            for p in range(TREES):
                G = c * TREES + p
                act.wait_ge(self.mask_done, G * 2 + 2)
                for leaf in range(2):
                    act.wait_ge(self.lg_ready, G * 2 + leaf + 1)
                    nc.scalar.activation(self.act[:, p % 2, leaf, :], self.lg[p % 2][leaf][:, :], ACT.Silu,
                                         bias=g.bin[:, 2 * p + leaf:2 * p + leaf + 1])\
                        .then_inc(self.silu_done, 1)
            act.wait_ge(self.out_done, c * TREES + TREES + 2)
            nc.scalar.activation(self.yrow[:, :], self.y[:, :], ACT.Copy).then_inc(self.y_taken, 1)

    def vector(self, nc, dve):
        g = self.g
        nc.vector.sem_inc(self.dec_done, 2)
        nc.vector.sem_inc(self.mask_done, 4)
        nc.vector.sem_inc(self.added, 1)
        with dve.Fori(0, NC) as c:
            for p in range(TREES + 1):
                if p < TREES:
                    G = c * TREES + p
                    dve.wait_ge(self.silu_done, G * 2 + 5)
                    dve.wait_ge(self.cnt_ready, G * 2 + 2)
                    nc.vector.tensor_scalar(self.dec[:, p % 2, :], self.lg[p % 2][0][:, :],
                                            g.bin[:, 2 * p:2 * p + 1], 0.0, ALU.add, ALU.is_gt)\
                        .then_inc(self.dec_done, 1)
                if p >= 1:
                    q = p - 1
                    G = c * TREES + q
                    dve.wait_ge(self.silu_done, G * 2 + 6)
                    dve.wait_ge(self.out_done, G + 1)
                    for leaf in range(2):
                        dve.wait_ge(self.cnt_ready, G * 2 + 5 + leaf)
                        nc.vector.scalar_tensor_tensor(
                            out=self.msk[:, q % 2, leaf, :], in0=self.cnt[leaf][:, :],
                            scalar=g.nright[:, leaf:leaf + 1], in1=self.act[:, q % 2, leaf, :],
                            op0=ALU.is_equal, op1=ALU.mult).then_inc(self.mask_done, 1)
            dve.wait_ge(self.y_turned, c + 1)
            nc.vector.tensor_tensor(g.x[:, bass.ds(c * TPC, TPC), :],
                                    self.yt[:, :].rearrange("p (t e) -> p t e", e=E),
                                    g.x[:, bass.ds(c * TPC, TPC), :], ALU.add).then_inc(self.added, 1)
        dve.wait_ge(self.added, NC + 1)


class Shared:
    pass


def hybrid_kernel(nc, t, out):
    with ExitStack() as ctx:
        def sb(name, shape, dt):
            return ctx.enter_context(nc.sbuf_tensor(name, shape, dt))

        def sem(name):
            return ctx.enter_context(nc.semaphore(name))

        g = Shared()
        g.bank = [ctx.enter_context(nc.psum_tensor(f"bank{i}", [P, C], F32)) for i in range(8)]
        g.w_q, g.w_up = t["w_q"], t["w_up"]

        x = sb("x", [P, NT, E], F32)
        xnT = sb("xnT", [P, T], F32)
        win = sb("win", [P, 2 * TREES, P], F32)
        wout = sb("wout", [P, 2 * TREES, E], F32)
        wob = sb("wob", [P, H * DB // P, E], F32)
        wa = sb("wa", [P, 5, E], F32)
        wdown = sb("wdown", [P, P], F32)
        wproj = sb("wproj", [P, 1, E], F32)
        ba = sb("ba", [P, 4], F32)
        bv = sb("bv", [P, E], F32)
        bproj = sb("bproj", [P, E], F32)
        bin_ = sb("bin", [P, 2 * TREES], F32)
        ident = sb("ident", [P, P], F32)
        identb = sb("identb", [P, P], BF16)
        masks = sb("masks", [P, 2, P], BF16)
        anc = sb("anc", [P, 2, P], BF16)
        nright = sb("nright", [P, 2], F32)
        stats = sb("stats", [P, NT, 6], F32)
        mv = sb("mv", [P, NT, 2], F32)
        ve = sb("ve", [P, NT], F32)
        std = sb("std", [P, NT], F32)
        rstd = sb("rstd", [P, NT], F32)
        mpart = sb("mpart", [P, NT, NC], F32)
        negm = sb("negm", [P, NT], F32)
        rcp = sb("rcp", [P, 2, TPC], F32)
        pb = sb("pb", [P, NB, C], F32)
        hi = sb("hi", [P, NB, C], F32R)
        lo = sb("lo", [P, NB, C], F32R)
        ot = sb("ot", [P, 2, C], F32)
        xn = sb("xn", [P, 2, C], F32)
        merge = sb("merge", [P, DA + 2], F32)
        g.x, g.xnT, g.win, g.wout, g.wa, g.wdown = x, xnT, win, wout, wa, wdown[:, :]
        g.ba, g.bv, g.bin = ba, bv[:, :], bin_
        g.ident, g.identb, g.mask_kq, g.mask_qk = ident[:, :], identb[:, :], masks[:, 0, :], masks[:, 1, :]
        g.anc, g.nright, g.stats, g.mv = anc, nright, stats, mv
        g.ve, g.std, g.rstd = ve[:, :], std[:, :], rstd[:, :]
        g.mpart, g.negm, g.rcp, g.pb = mpart[:, :, :], negm[:, :], rcp, pb
        g.hi, g.lo, g.ot, g.xn, g.merge_a = hi, lo, ot, xn, merge[0:Attention.VM, :]
        g.spill = nc.dram_tensor("qk_parts", (2, PARTS, E, T), BF16, kind="Internal").ap()
        g.att_dram = nc.dram_tensor("att_b", (T, H * DB), F32, kind="Internal").ap()\
            .rearrange("(t p) c -> p t c", p=P)

        g.x_in = sem("x_in")
        g.w_in = sem("w_in")
        g.w_late = sem("w_late")
        g.stored = sem("stored")
        first = [(ident[:, :], t["ident"]), (wa[:, :, :], t["wa"]), (ba[:, :], t["ba"]), (bv[:, :], t["bv"]),
                 (identb[:, :], t["identb"]), (masks[:, :, :], t["masks"]), (merge[:, :], t["merge"])]
        later = [(wproj[:, 0, :], t["wproj"]), (bproj[:, :], t["bproj"]),
                 (win[:, :, :], t["win"]), (wout[:, :, :], t["wout"]), (bin_[:, :], t["bin"]),
                 (anc[:, :, :], t["anc"]), (nright[:, :], t["nright"]),
                 (wdown[:, :], t["w_down"]), (wob[:, :, :], t["w_out"])]

        ln = [Norm(f"ln{i}", sem, g) for i in range(4)]

        with ExitStack() as own:
            def sb(name, shape, dt):
                return own.enter_context(nc.sbuf_tensor(name, shape, dt))
            att = AttentionA("a", sem, g, sb)
            proj = OutProj("pa", sem, g, sb, 1, att.att, wproj, bproj[:, :], [(att.norm_done, H * NC + 2)])
            block = own.enter_context(nc.Block())

            @block.sync
            def _(sp):
                sp.dma_start(x[:, :, :], t["x"][0].rearrange("(t p) e -> p t e", p=P)).then_inc(g.x_in, 16)
                for dst, src in first:
                    sp.dma_start(dst, src).then_inc(g.w_in, 16)
                sp.dma_start(att.tables[:, 0, :], t["cos"]).then_inc(att.tables_in, 16)
                sp.dma_start(att.tables[:, 1, :], t["sin"]).then_inc(att.tables_in, 16)
                for dst, src in later:
                    sp.dma_start(dst, src).then_inc(g.w_late, 16)
                sp.sem_inc(att.rows_in, att.ROWS)
                sp.wait_ge(att.consts, 1)
                att.sync_spill(sp)
                att.run(sp, lambda *a: att.sync_step(nc, sp, *a))
                sp.wait_ge(g.w_late, 16 * len(later))

            @block.vector
            def _(dve):
                dve.wait_ge(g.x_in, 16)
                ln[0].vector(nc, dve)
                dve.wait_ge(g.w_in, 16 * len(first))
                att.vector_credits(nc)
                att.vector_project(nc, dve)
                att.run(dve, lambda *a: att.vector_step(nc, dve, *a))
                att.vector_end(nc, dve)
                proj.vector(nc, dve)

            @block.gpsimd
            def _(pool):
                att.run(pool, lambda *a: att.pool_step(nc, pool, *a))

            @block.scalar
            def _(act):
                ln[0].scalar(nc, act)
                att.scalar_credits(nc)
                att.run(act, lambda *a: att.scalar_step(nc, act, *a))
                att.scalar_end(nc, act)
                proj.scalar(nc, act)

            @block.tensor
            def _(pe):
                pe.wait_ge(g.w_in, 16 * len(first))
                ln[0].tensor(nc, pe)
                att.tensor_credits(nc)
                att.tensor_project(nc, pe, ln[0])
                att.run(pe, lambda *a: att.tensor_step(nc, pe, *a))
                att.tensor_end(nc, pe)
                pe.wait_ge(g.w_late, 16 * len(later))
                proj.tensor(nc, pe)

        def feed_forward(i, norm):
            with ExitStack() as own:
                def sb(name, shape, dt):
                    return own.enter_context(nc.sbuf_tensor(name, shape, dt))
                ffn = TreeFFN(f"f{i}", sem, g, sb)
                block = own.enter_context(nc.Block())

                @block.vector
                def _(dve):
                    norm.vector(nc, dve)
                    ffn.vector(nc, dve)

                @block.scalar
                def _(act):
                    norm.scalar(nc, act)
                    ffn.scalar(nc, act)

                @block.tensor
                def _(pe):
                    norm.tensor(nc, pe)
                    ffn.tensor(nc, pe, norm)

                @block.sync
                def _(sp):
                    if i == 1:
                        sp.wait_ge(ffn.added, NC + 1)
                        sp.dma_start(out[0].rearrange("(t p) e -> p t e", p=P), x[:, :, :])\
                            .then_inc(g.stored, 16)
                        sp.wait_ge(g.stored, 16)

        feed_forward(0, ln[1])

        with ExitStack() as own:
            def sb(name, shape, dt):
                return own.enter_context(nc.sbuf_tensor(name, shape, dt))
            att_b = AttentionB("b", sem, g, sb)
            proj_b = OutProj("pb", sem, g, sb, H * DB // P, g.att_dram, wob, None,
                             [(done, 16 * (H * NC // 2 + 1)) for done in att_b.stored])
            block = own.enter_context(nc.Block())

            @block.sync
            def _(sp):
                sp.sem_inc(att_b.rows_in, att_b.ROWS)
                for done in att_b.stored:
                    sp.sem_inc(done, 16)
                sp.wait_ge(att_b.consts, 1)
                att_b.run(sp, lambda *a: att_b.sync_step(nc, sp, *a))
                att_b.store_chunk(sp, H - 1, NC - 1)
                proj_b.sync(sp)

            @block.vector
            def _(dve):
                ln[2].vector(nc, dve)
                att_b.vector_credits(nc)
                att_b.vector_project(nc, dve)
                att_b.run(dve, lambda *a: att_b.vector_step(nc, dve, *a))
                att_b.vector_end(nc, dve)
                proj_b.vector(nc, dve)

            @block.gpsimd
            def _(pool):
                att_b.run(pool, lambda *a: att_b.pool_step(nc, pool, *a))

            @block.scalar
            def _(act):
                ln[2].scalar(nc, act)
                att_b.scalar_credits(nc)
                att_b.scalar_project(nc, act)
                att_b.run(act, lambda *a: att_b.scalar_step(nc, act, *a))
                att_b.scalar_end(nc, act)

            @block.tensor
            def _(pe):
                ln[2].tensor(nc, pe)
                att_b.tensor_credits(nc)
                att_b.tensor_project(nc, pe, ln[2])
                att_b.run(pe, lambda *a: att_b.tensor_step(nc, pe, *a))
                att_b.tensor_end(nc, pe)
                proj_b.tensor(nc, pe)

        feed_forward(1, ln[3])


def rope_tables(np):
    pos = np.arange(T, dtype=np.float32)
    inv = (1.0 / np.float32(10000.0) ** (np.arange(0, DA, 2, dtype=np.float32) / np.float32(DA))).astype(np.float32)
    freqs = inv[:, None] * pos[None, :]
    cos = np.repeat(np.cos(freqs), 2, axis=0)
    sin = np.repeat(np.sin(freqs), 2, axis=0) * np.tile(np.array([-1.0, 1.0], np.float32), DA // 2)[:, None]
    return (np.ascontiguousarray(np.tile(a, (H, 1)).astype(np.float32)) for a in (cos, sin))


def tree_tables(np):
    inner = 2 ** DEPTH - 1
    anc = np.zeros((P, 2, P), np.float32)
    right = np.zeros((P, 2), np.float32)
    for node in range(2 * inner + 1):
        leaf, col = (0, node) if node < inner else (1, node - inner)
        at = node
        while at > 0:
            up, step = (at - 1) // 2, 1 if at % 2 == 0 else -1
            anc[up, leaf, col] = step
            right[col, leaf] += step == 1
            at = up
    return anc, right


def kernel(**inputs):
    import numpy as np
    import ml_dtypes
    import concourse.bacc as bacc
    from concourse.bass_utils import run_bass_kernel_spmd as run

    a = {k: np.asarray(v) for k, v in inputs.items()}
    inner, nodes = 2 ** DEPTH - 1, 2 ** (DEPTH + 1) - 1
    bf16 = ml_dtypes.bfloat16
    cos, sin = rope_tables(np)
    anc, right = tree_tables(np)
    turned = np.arange(E) ^ 1
    W, b = a["L0_attn_a_Wqkv"], a["L0_attn_a_bqkv"]
    wq, wk, wv = W[:, :E], W[:, E:2 * E], W[:, 2 * E:]
    bq, bk, bv = b[:E], b[E:2 * E], b[2 * E:]

    def by_tree(w):
        w = w.reshape(TREES, nodes, *w.shape[1:])
        full = np.zeros((P, TREES, 2) + w.shape[2:], w.dtype)
        full[:inner, :, 0] = np.swapaxes(w[:, :inner], 0, 1)
        full[:, :, 1] = np.swapaxes(w[:, inner:], 0, 1)
        return full.reshape((P, 2 * TREES) + w.shape[2:])

    merge = np.zeros((P, DA + 2), np.float32)
    merge[np.arange(2 * DA), np.arange(2 * DA) % DA] = 1
    merge[2 * DA, DA] = 1
    rows = np.arange(P)
    masks = np.zeros((P, 2, P), np.float32)
    masks[:, 0][rows[:, None] > rows[None, :]] = NEG
    masks[:, 1][rows[None, :] > rows[:, None]] = NEG
    arrays = {
        "x": a["L0_attn_a_x"],
        "wa": np.stack([wq, wq[:, turned], wk, wk[:, turned], wv], axis=1),
        "ba": np.stack([bq, bq[turned], bk, bk[turned]], axis=1),
        "bv": np.broadcast_to(bv, (P, E)),
        "wproj": a["L0_attn_a_Wproj"],
        "bproj": np.broadcast_to(a["L0_attn_a_bproj"], (P, E)),
        "w_down": a["L0_attn_b_w_kv_down"],
        "w_up": a["L0_attn_b_w_kv_up"],
        "w_q": a["L0_attn_b_w_q"],
        "w_out": a["L0_attn_b_w_out"].reshape(H * DB // P, P, E).transpose(1, 0, 2),
        "win": by_tree(a["L0_ffn_W_in"]).transpose(2, 1, 0),
        "bin": by_tree(a["L0_ffn_b_in"]),
        "wout": by_tree(a["L0_ffn_W_out"].T),
        "ident": np.eye(P, dtype=np.float32),
        "identb": np.eye(P, dtype=np.float32).astype(bf16),
        "masks": masks.astype(bf16),
        "anc": anc.astype(bf16),
        "nright": right,
        "merge": merge,
        "cos": cos,
        "sin": sin,
    }
    nc = bacc.Bacc("TRN2", target_bir_lowering=False, num_devices=1)
    arrays = {k: np.ascontiguousarray(v) for k, v in arrays.items()}
    aps = {k: nc.dram_tensor(f"in_{k}", v.shape, mybir.dt.from_np(v.dtype), kind="ExternalInput").ap()
           for k, v in arrays.items()}
    out = nc.dram_tensor("out", (1, T, E), F32, kind="ExternalOutput").ap()
    hybrid_kernel(nc, aps, out)
    r = run(nc, [{f"in_{k}": v for k, v in arrays.items()}], core_ids=[0])
    return r.results[0]["out"]
```

```python
from contextlib import ExitStack

import concourse.bass as bass
from concourse import mybir

F32 = mybir.dt.float32
F32R = mybir.dt.float32r
BF16 = mybir.dt.bfloat16
ALU = mybir.AluOpType
ACT = mybir.ActivationFunctionType
AX = mybir.AxisListType

P = 128
T = 2048
E = 128
NT = T // P
C = 512
NC = T // C
TPC = C // P
H = 16
DA = E // H
DB = 64
EPS = 1e-5
NEG = -1e30
LOWEST = -3e38
TREES = 8
DEPTH = 7
PARTS = 3

UNITS = [(j, kt) for j in range(NC) for kt in range(TPC * (j + 1))]
PIECES = [(i, ch) for i in range(NT) for ch in range(i // TPC + 1)]
NU = len(UNITS)
NP = len(PIECES)
LAST_UNIT = {j: max(n for n, u in enumerate(UNITS) if u[0] == j) for j in range(NC)}
V_AT = 6
PV_LAG = 4
NB = 5
assert NU % NB == 0 and NU % 2 == 0 and NC % 2 == 0


PAIRS = [(0, 0), (0, 1), (0, 2), (1, 0), (1, 1), (2, 0)]


class Chain:

    def __init__(self, eng, sem):
        self.eng, self.sem, self.n = eng, sem, 0

    def link(self, ins):
        ins.then_inc(self.sem, 1)
        self.n += 1
        self.eng.wait_ge(self.sem, self.n)


class Norm:

    def __init__(self, name, sem, g):
        self.g = g
        self.hi_ready = sem(f"{name}_hi_ready")
        self.var_ready = sem(f"{name}_var_ready")
        self.std_ready = sem(f"{name}_std_ready")
        self.rows_ready = sem(f"{name}_rows_ready")
        self.turned = sem(f"{name}_turned")
        self.xT_ready = sem(f"{name}_xT_ready")
        self.own = sem(f"{name}_own")

    def lo_part(self, nc, dve, xnT, c):
        cols = slice(c * C, (c + 1) * C)
        dve.wait_ge(self.hi_ready, c + 1)
        nc.vector.tensor_tensor(xnT[1][:, cols], self.g.bank[c % 2][:, :],
                                xnT[0][:, cols].bitcast(F32), ALU.subtract).then_inc(self.xT_ready, 1)

    def vector(self, nc, dve, xnT):
        g, chain = self.g, Chain(dve, self.own)
        for t in range(NT):
            last = nc.vector.bn_stats(g.stats[:, t, :], g.x[:, t, :])
        chain.link(last)
        for t in range(NT):
            last = nc.vector.bn_aggr(g.mv[:, t, :], g.stats[:, t, :])
        chain.link(last)
        nc.vector.tensor_scalar(g.ve, g.mv[:, :, 1], EPS, None, ALU.add).then_inc(self.var_ready, 1)
        dve.wait_ge(self.std_ready, 1)
        chain.link(nc.vector.reciprocal(g.rstd, g.std))
        for c in range(NC):
            if c >= 2:
                dve.wait_ge(self.turned, c - 1)
            for t in range(TPC):
                n = TPC * c + t
                last = nc.vector.tensor_scalar(g.xn[:, c % 2, t * P:(t + 1) * P], g.x[:, n, :],
                                               g.mv[:, n, 0:1], g.rstd[:, n:n + 1],
                                               ALU.subtract, ALU.mult)
            last.then_inc(self.rows_ready, 1)
            if c >= 1 and len(xnT) == 2:
                self.lo_part(nc, dve, xnT, c - 1)
        if len(xnT) == 2:
            self.lo_part(nc, dve, xnT, NC - 1)

    def scalar(self, nc, act, xnT):
        g = self.g
        act.wait_ge(self.var_ready, 1)
        nc.scalar.activation(g.std, g.ve, ACT.Sqrt).then_inc(self.std_ready, 1)
        for c in range(NC):
            act.wait_ge(self.turned, c + 1)
            nc.scalar.activation(xnT[0][:, c * C:(c + 1) * C], g.bank[c % 2][:, :], ACT.Copy)\
                .then_inc(self.hi_ready if len(xnT) == 2 else self.xT_ready, 1)

    def tensor(self, nc, pe):
        g = self.g
        for c in range(NC):
            pe.wait_ge(self.rows_ready, c + 1)
            if c >= 2:
                pe.wait_ge(self.xT_ready, c - 1)
            for t in range(TPC):
                last = nc.tensor.transpose(g.bank[c % 2][:, t * P:(t + 1) * P],
                                           g.xn[:, c % 2, t * P:(t + 1) * P], g.ident)
            last.then_inc(self.turned, 1)


class Attention:

    TAKE_LAG, TURN_LAG, NORM_LAG = PV_LAG + 1, PV_LAG + 2, PV_LAG + 4
    FIRST_MAX, END_MAX, TURN = 8, 34, 35
    LO_LAG = 2
    ROWS = None
    ST_CREDIT = 1
    VM = 66

    def __init__(self, name, sem, g):
        self.g = g
        self.st_ready = sem(f"{name}_scores_ready")
        self.exp_done = sem(f"{name}_exp_done")
        self.hi_done = sem(f"{name}_hi_done")
        self.lo_dve = sem(f"{name}_lo_dve")
        self.lo_pool = sem(f"{name}_lo_pool")
        self.pv_done = sem(f"{name}_pv_done")
        self.ot_taken = sem(f"{name}_ot_taken")
        self.tr_ready = sem(f"{name}_tr_ready")
        self.norm_done = sem(f"{name}_norm_done")
        self.mx_ready = sem(f"{name}_mx_ready")
        self.mx_done = sem(f"{name}_mx_done")
        self.negm_ready = sem(f"{name}_negm_ready")
        self.mt_ready = sem(f"{name}_mt_ready")
        self.mt_taken = sem(f"{name}_mt_taken")
        self.rows_in = sem(f"{name}_rows_in")
        self.own = sem(f"{name}_own")
        self.row_own = sem(f"{name}_row_own")
        self.consts = sem(f"{name}_consts")
        B = g.bank
        self.st, self.sm, self.pv, self.aux = B[0:2], B[2:4], B[4:6], B[6]
        self.tr = B[7][:, 0:TPC * self.VM].rearrange("p (t d) -> p t d", d=self.VM)
        self.lo_units = {"dve": [n for n in self.SPLIT if n not in self.LO_ON_POOL],
                         "pool": [n for n in self.SPLIT if n in self.LO_ON_POOL]}

    def pieces_at(self, n):
        span, at = self.END_MAX - self.FIRST_MAX, n - self.FIRST_MAX
        return range(at * NP // span, (at + 1) * NP // span) if 0 <= at < span else range(0)

    def offset(self, n):
        j, kt = UNITS[n]
        return max(0, kt - TPC * j) * P

    def wait_hi(self, eng, s, n):
        eng.wait_ge(self.hi_done, s * len(self.SPLIT) + self.SPLIT.index(n) + 1)

    def wait_lo(self, eng, s, n):
        for who, done in (("dve", self.lo_dve), ("pool", self.lo_pool)):
            mine = self.lo_units[who]
            if n % NU in mine:
                at = mine.index(n % NU) + 1 - (len(mine) if n < 0 else 0)
                eng.wait_ge(done, s * len(mine) + at + NB)

    def hi_part(self, nc, act, s, n):
        g, off = self.g, self.offset(n)
        act.wait_ge(self.exp_done, s * NU + n + 3)
        act.wait_ge(self.pv_done, s * NU + n + 1)
        nc.scalar.activation(g.hi[:, n % NB, off:C], g.pb[:, n % NB, off:C], ACT.Copy)\
            .then_inc(self.hi_done, 1)

    def lo_part(self, nc, eng, s, n):
        g, off = self.g, self.offset(n)
        on_pool = n in self.lo_units["pool"]
        self.wait_hi(eng, s, n)
        where = nc.gpsimd if on_pool else nc.vector
        where.tensor_tensor(g.lo[:, n % NB, off:C], g.pb[:, n % NB, off:C],
                            g.hi[:, n % NB, off:C].bitcast(F32), ALU.subtract)\
            .then_inc(self.lo_pool if on_pool else self.lo_dve, 1)

    def pool_step(self, nc, pool, s, main, prep, before):
        if main:
            for n in self.lo_units["pool"]:
                self.lo_part(nc, pool, s, n)

    def vector_credits(self, nc):
        nc.vector.sem_inc(self.norm_done, 2)
        nc.vector.sem_inc(self.ot_taken, 2)
        nc.vector.sem_inc(self.mx_done, 2)
        nc.vector.sem_inc(self.mt_taken, 1)
        nc.vector.sem_inc(self.lo_dve, NB)
        nc.vector.sem_inc(self.lo_pool, NB)

    def vector_lo(self, nc, dve, s, n):
        if n in self.lo_units["dve"]:
            self.lo_part(nc, dve, s, n)

    def vector_step(self, nc, dve, s, main, prep, before):
        g, D, hp = self.g, self.D, s + 1
        for n in range(NU):
            if before and n < self.LO_LAG:
                self.vector_lo(nc, dve, s - 1, NU + n - self.LO_LAG)
            if main and n >= self.LO_LAG:
                self.vector_lo(nc, dve, s, n - self.LO_LAG)
            if prep:
                for m in self.pieces_at(n):
                    i, ch = PIECES[m]
                    w = self.piece_width(m)
                    dve.wait_ge(self.mx_ready, hp * NP + m + 1)
                    nc.vector.tensor_reduce(g.mpart[:, i, ch:ch + 1], self.sm[m % 2][:, 0:w],
                                            axis=AX.X, op=ALU.max).then_inc(self.mx_done, 1)
                    if m == NP - 1:
                        dve.wait_ge(self.mx_done, hp * NP + NP + 2)
                        nc.vector.tensor_reduce(g.negm, g.mpart, axis=AX.X, op=ALU.max,
                                                negate=True).then_inc(self.negm_ready, 1)
                if n >= 1:
                    self.vector_prepare(nc, dve, s, n - 1)
                if n == self.TURN:
                    dve.wait_ge(self.mt_ready, hp + 1)
                    dve.wait_ge(self.rows_in, self.ROWS * (hp + 1))
                    self.take_rows(nc, dve, hp)
            self.for_ends(s, n, self.TAKE_LAG, main, before, lambda *a: self.take_chunk(nc, dve, *a))
            self.for_ends(s, n, self.NORM_LAG, main, before, lambda *a: self.normalise(nc, dve, *a))

    def vector_end(self, nc, dve):
        for n in range(NU - self.LO_LAG, NU):
            self.vector_lo(nc, dve, H - 1, n)
        self.take_chunk(nc, dve, H - 1, NC - 1)
        self.normalise(nc, dve, H - 1, NC - 1)

    def for_ends(self, s, n, lag, main, before, do):
        for j in range(NC):
            if main and n - lag == LAST_UNIT[j]:
                do(s, j)
            if before and n - lag + NU == LAST_UNIT[j]:
                do(s - 1, j)

    def take_chunk(self, nc, dve, s, j):
        dve.wait_ge(self.pv_done, s * NU + LAST_UNIT[j] + 1 + NB)
        dve.wait_ge(self.tr_ready, s * NC + j + 1)
        nc.vector.tensor_copy(self.g.ot[0:self.VM, j % 2, :], self.pv[j % 2][0:self.VM, :])\
            .then_inc(self.ot_taken, 1)

    def normalise(self, nc, dve, s, j):
        g, D = self.g, self.D
        dve.wait_ge(self.tr_ready, s * NC + j + 3)
        dve.wait_ge(self.norm_done, s * NC + j + 1)
        self.wait_att(dve, s, j)
        sums, values = self.sums_and_values(nc)
        nc.vector.reciprocal(g.rcp[:, j % 2, :], sums).then_inc(self.own, 1)
        dve.wait_ge(self.own, s * NC + j + 1)
        nc.vector.tensor_tensor(self.att_out(s, j), values,
                                g.rcp[:, j % 2, :].unsqueeze(2).to_broadcast([P, TPC, D]),
                                ALU.mult).then_inc(self.norm_done, 1)

    def scalar_credits(self, nc):
        nc.scalar.sem_inc(self.exp_done, 2)

    def scalar_step(self, nc, act, s, main, prep, before):
        g = self.g
        for n in range(NU):
            off = self.offset(n)
            if main:
                act.wait_ge(self.st_ready, s * NU + n + 1 + self.ST_CREDIT)
                if (n - NB) % NU in self.SPLIT:
                    self.wait_lo(act, s, n - NB)
                else:
                    act.wait_ge(self.pv_done, s * NU + n + 1)
                nc.scalar.activation(g.pb[:, n % NB, off:C], self.st[n % 2][:, off:C], ACT.Exp,
                                     scale=self.D ** -0.5).then_inc(self.exp_done, 1)
                if n - 1 in self.SPLIT:
                    self.hi_part(nc, act, s, n - 1)
            if before and n == 0:
                self.hi_last(nc, act, s - 1)
            if prep:
                self.scalar_prepare(nc, act, s, n)

    def hi_last(self, nc, act, s):
        if NU - 1 in self.SPLIT:
            self.hi_part(nc, act, s, NU - 1)

    def scalar_end(self, nc, act):
        self.hi_last(nc, act, H - 1)

    def tensor_credits(self, nc):
        nc.tensor.sem_inc(self.st_ready, self.ST_CREDIT)
        nc.tensor.sem_inc(self.pv_done, NB)
        nc.tensor.sem_inc(self.tr_ready, 2)

    def piece_width(self, m):
        i, ch = PIECES[m]
        return min(C, (i + 1) * P - ch * C)

    def tensor_step(self, nc, pe, s, main, prep, before):
        g, b, hp = self.g, self.par, s + 1
        for n, (j, kt) in enumerate(UNITS):
            if main:
                if n == 0:
                    pe.wait_ge(self.rows_in, self.ROWS * (s + 2))
                off = self.offset(n)
                pe.wait_ge(self.exp_done, s * NU + n + 1)
                out = self.st[n % 2]
                pairs = self.main_pairs[b]
                for i, (k, q) in enumerate(pairs):
                    mm = nc.tensor.matmul(out[:, off:C], k[:, kt * P:(kt + 1) * P],
                                          q[:, j * C + off:(j + 1) * C], start=i == 0,
                                          stop=i == len(pairs) - 1 and kt < TPC * j)
                if kt >= TPC * j:
                    mm = nc.tensor.matmul(out[:, off:off + P], g.identb, g.mask_kq,
                                          start=False, stop=True)
                mm.then_inc(self.st_ready, 1)
            if prep:
                self.tensor_prepare(nc, pe, s, n)
                for m in self.pieces_at(n):
                    i, ch = PIECES[m]
                    if i % TPC == 0 and ch == 0:
                        self.wait_operands(pe, hp, i // TPC)
                    w = self.piece_width(m)
                    pe.wait_ge(self.mx_done, hp * NP + m + 1)
                    out = self.sm[m % 2]
                    last = ch == i // TPC
                    mm = nc.tensor.matmul(out[:, 0:w], self.q_max[1 - b][:, i * P:(i + 1) * P],
                                          self.k_max[1 - b][:, ch * C:ch * C + w],
                                          start=True, stop=not last)
                    if last:
                        mm = nc.tensor.matmul(out[:, w - P:w], g.identb, g.mask_qk,
                                              start=False, stop=True)
                    mm.then_inc(self.mx_ready, 1)
                if n == self.TURN:
                    pe.wait_ge(self.negm_ready, hp + 1)
                    pe.wait_ge(self.mt_taken, hp + 1)
                    self.wait_turn_bank(pe, hp)
                    nc.tensor.transpose(self.aux[0:NT, 0:P], g.negm, g.ident)\
                        .then_inc(self.mt_ready, 1)
            if before and n < PV_LAG:
                self.pv_unit(nc, pe, s - 1, NU + n - PV_LAG, 1 - b)
            if main and n >= PV_LAG:
                self.pv_unit(nc, pe, s, n - PV_LAG, b)
            self.for_ends(s, n, self.TURN_LAG, main, before, lambda *a: self.turn_chunk(nc, pe, *a))

    def tensor_end(self, nc, pe):
        for n in range(NU - PV_LAG, NU):
            self.pv_unit(nc, pe, H - 1, n, 1)
        self.turn_chunk(nc, pe, H - 1, NC - 1)

    def turn_chunk(self, nc, pe, s, j):
        pe.wait_ge(self.ot_taken, s * NC + j + 3)
        pe.wait_ge(self.norm_done, s * NC + j + 2)
        for ql in range(TPC):
            ot = self.g.ot[0:self.VM, j % 2, ql * P:(ql + 1) * P]
            mm = nc.tensor.transpose(self.tr[:, ql, :], ot, self.g.ident[0:self.VM, 0:self.VM])
        mm.then_inc(self.tr_ready, 1)

    def pv_unit(self, nc, pe, s, n, b):
        g, VM = self.g, self.VM
        j, kt = UNITS[n]
        if n == 0:
            self.wait_values(pe, s)
        if kt == 0:
            pe.wait_ge(self.ot_taken, s * NC + j + 1)
        off = self.offset(n)
        if n in self.SPLIT:
            self.wait_lo(pe, s, n)
            prods = self.value_products(b, kt, g.hi[:, n % NB, off:C], g.lo[:, n % NB, off:C])
        else:
            pe.wait_ge(self.exp_done, s * NU + n + 3)
            prods = [(self.vf[b][:, kt, :], g.pb[:, n % NB, off:C])]
        for i, (v, e) in enumerate(prods):
            mm = nc.tensor.matmul(self.pv[j % 2][0:v.shape[1], off:C], v, e, start=kt == 0 and i == 0,
                                  stop=n == LAST_UNIT[j] and i == len(prods) - 1,
                                  skip_group_check=True)
        mm.then_inc(self.pv_done, 1)

    def run(self, eng, step):
        self.par = 1
        step(-1, False, True, False)
        self.par = 0
        step(0, True, True, False)
        with eng.Fori(0, H // 2 - 1) as u:
            self.par = 1
            step(u * 2 + 1, True, True, True)
            self.par = 0
            step(u * 2 + 2, True, True, True)
        self.par = 1
        step(H - 1, True, False, True)


class AttentionA(Attention):
    D = DA
    KM = len(PAIRS) * DA
    KB = KM + PARTS
    ROWS = 16 * PARTS
    STAGE = 16 * 2
    SPLIT = [n for n in range(NU) if n % 10 not in (1, 5, 8)]
    assert {n for n, (_, kt) in enumerate(UNITS) if kt == 0} <= set(SPLIT)
    LO_ON_POOL = [n for n in range(1, NU) if n % 10 != 4]
    FIRST_MAX, END_MAX, TURN = 6, 33, 33
    TAKE_LAG, TURN_LAG, NORM_LAG = PV_LAG, PV_LAG + 1, PV_LAG + 2

    def __init__(self, name, sem, g, sb):
        super().__init__(name, sem, g)
        self.tables = sb("a_tables", [P, 2, T], F32)
        self.split = [sb(f"a_split{i}", [P, PARTS, T], BF16) for i in range(2)]
        self.stack = [[sb(f"a_stack{i}{j}", [P, T], BF16) for j in range(2)] for i in range(2)]
        self.vall = sb("a_vall", [P, NT, H, 2, DA], F32R)
        self.att = sb("a_att", [P, NT, E], F32)
        self.v = [sb(f"a_v{i}", [P, NT, self.VM], F32R) for i in range(2)]
        self.vwhole = sb("a_vwhole", [P, NT, E], F32)
        self.vf = [sb(f"a_vf{i}", [P, NT, 2 * DA + 2], F32) for i in range(2)]
        self.tmp = sb("a_tmp", [P, 2, 3, C], F32)
        self.res = sb("a_res", [P, 2, 2, C], F32)
        self.mrow = sb("a_mrow", [P, 3, P], F32)
        self.both = sb("a_both", [P, TPC, DA], F32)
        self.mparts = sb("a_mparts", [P, PARTS, P], BF16)
        q, k = self.stack
        self.main_pairs = [[(k[i][0:self.KB], q[i][0:self.KB])] for i in range(2)]
        self.q_max, self.k_max = [a[0:self.KM] for a in q], [a[0:self.KM] for a in k]
        self.tables_in = sem(f"{name}_tables_in")
        self.proj_ready = sem(f"{name}_proj_ready")
        self.rotated = sem(f"{name}_rotated")
        self.part_done = [sem(f"{name}_part{i}_done") for i in range(PARTS)]
        self.rest_done = [sem(f"{name}_rest{i}_done") for i in range(2)]
        self.vproj_ready = sem(f"{name}_vproj_ready")
        self.vproj_taken = sem(f"{name}_vproj_taken")
        self.staged = sem(f"{name}_staged")
        self.spilled = sem(f"{name}_spilled")
        self.v_ready = sem(f"{name}_v_ready")
        self.rope_own = sem(f"{name}_rope_own")

    def att_out(self, s, j):
        return self.att[:, TPC * j:TPC * (j + 1), bass.ds(s * DA, DA)]

    def wait_att(self, dve, s, j):
        pass

    def value_products(self, b, kt, hi, lo):
        v = self.v[b][:, kt, :]
        return [(v, hi), (v, lo)]

    def sums_and_values(self, nc):
        nc.vector.tensor_reduce(self.both[:, :, :],
                                self.tr[:, :, 0:2 * DA].rearrange("p t (c d) -> p t d c", c=2),
                                axis=AX.X, op=ALU.add)
        return self.tr[:, :, 2 * DA], self.both[:, :, :]

    def tensor_project(self, nc, pe, ln):
        g = self.g
        n = 0
        pe.wait_ge(ln.xT_ready, NC)
        for which in range(2):
            for c in range(NC):
                if n >= 2:
                    pe.wait_ge(self.rotated, n - 1)
                for turned in range(2):
                    mm = nc.tensor.matmul(g.bank[2 * (n % 2) + turned][:, :],
                                          g.wa[:, 2 * which + turned, :], g.xnT[:, c * C:(c + 1) * C],
                                          start=True, stop=True)
                mm.then_inc(self.proj_ready, 1)
                n += 1
        for c in range(NC):
            if c >= 2:
                pe.wait_ge(self.vproj_taken, c - 1)
            for t in range(TPC):
                mm = nc.tensor.matmul(g.bank[4 + c % 2][:, t * E:(t + 1) * E],
                                      g.xnT[:, (c * TPC + t) * P:(c * TPC + t + 1) * P],
                                      g.wa[:, 4, :], start=True, stop=True)
            mm.then_inc(self.vproj_ready, 1)

    def vector_project(self, nc, dve):
        g, chain = self.g, Chain(dve, self.rope_own)
        for i in range(2):
            chain.link(nc.vector.memset(self.stack[1][i][32:self.KB, :], 1.0))
            chain.link(nc.vector.memset(self.v[i][:, :, :].bitcast(F32), 0.0))
            chain.link(nc.vector.memset(self.v[i][:, :, 2 * DA:2 * DA + 1].bitcast(F32), 1.0))
            chain.link(nc.vector.memset(self.vf[i][:, :, :], 0.0))
            chain.link(nc.vector.memset(self.vf[i][:, :, 2 * DA:2 * DA + 1], 1.0))
        nc.vector.memset(g.mpart, LOWEST).then_inc(self.consts, 1)
        dve.wait_ge(self.consts, 1)
        dve.wait_ge(self.tables_in, 32)
        for n in range(2 * NC + 2):
            if n < 2 * NC:
                which, c = divmod(n, NC)
                tmp = self.tmp[:, n % 2]
                dve.wait_ge(self.proj_ready, n + 1)
                if n >= 2:
                    dve.wait_ge(self.rest_done[0], n - 1)
                for turned in range(2):
                    ins = nc.vector.scalar_tensor_tensor(
                        out=tmp[:, turned, :], in0=g.bank[2 * (n % 2) + turned][:, :],
                        scalar=g.ba[:, 2 * which + turned:2 * which + turned + 1],
                        in1=self.tables[:, turned, c * C:(c + 1) * C], op0=ALU.add, op1=ALU.mult)
                chain.link(ins)
                nc.vector.tensor_tensor(tmp[:, 2, :], tmp[:, 0, :], tmp[:, 1, :], ALU.add)\
                    .then_inc(self.rotated, 1)
            for i in range(2):
                m = n - 1 - i
                if 0 <= m < 2 * NC:
                    dve.wait_ge(self.part_done[i], m + 1)
                    if m >= 2:
                        dve.wait_ge(self.rest_done[1] if i == 0 else self.part_done[2], m - 1)
                    nc.vector.tensor_tensor(self.res[:, m % 2, i, :], self.whole(m, i), self.part(m, i),
                                            ALU.subtract).then_inc(self.rest_done[i], 1)
        for c in range(NC):
            dve.wait_ge(self.vproj_ready, c + 1)
            tiles = slice(c * TPC, (c + 1) * TPC)
            rows = self.vwhole[:, tiles, :].rearrange("p t (h d) -> p t h d", h=H, d=DA)
            chain.link(nc.vector.tensor_tensor(
                self.vwhole[:, tiles, :],
                g.bank[4 + c % 2][:, :].rearrange("p (t e) -> p t e", e=E),
                g.bv.unsqueeze(1).to_broadcast([P, TPC, E]), ALU.add))
            hi, lo = self.vall[:, tiles, :, 0, :], self.vall[:, tiles, :, 1, :]
            chain.link(nc.vector.tensor_copy(hi, rows))
            nc.vector.tensor_tensor(lo, rows, hi.bitcast(F32), ALU.subtract).then_inc(self.vproj_taken, 1)

    def part(self, m, i):
        which, c = divmod(m, NC)
        return self.split[which][:, i, c * C:(c + 1) * C]

    def whole(self, m, i):
        return self.tmp[:, m % 2, 2, :] if i == 0 else self.res[:, m % 2, i - 1, :]

    def scalar_project(self, nc, act):
        for n in range(2 * NC + 2):
            for i in range(PARTS):
                m = n - i
                if 0 <= m < 2 * NC:
                    act.wait_ge(self.rotated if i == 0 else self.rest_done[i - 1], m + 1)
                    nc.scalar.activation(self.part(m, i), self.whole(m, i), ACT.Copy)\
                        .then_inc(self.part_done[i], 1)

    def vector_prepare(self, nc, dve, s, n):
        pass

    def sync_spill(self, sp):
        for which in range(2):
            sp.wait_ge(self.part_done[2], NC * (which + 1))
            for i, pair in enumerate(PAIRS):
                sp.dma_start(self.g.spill[which, i], self.split[which][:, pair[which], :])\
                    .then_inc(self.spilled, 16)
        sp.wait_ge(self.spilled, 16 * 2 * len(PAIRS))

    def sync_step(self, nc, sp, s, main, prep, before):
        if not prep:
            return
        hp, b = s + 1, 1 - self.par
        if main:
            sp.wait_ge(self.st_ready, s * NU + self.ST_CREDIT)
        for which in (1, 0):
            sp.dma_start(self.stack[which][b][0:self.KM, :], self.g.spill[which, :, bass.ds(hp * DA, DA), :])\
                .then_inc(self.staged, 16)
        sp.wait_ge(self.mt_taken, hp + 2)
        for r in range(PARTS):
            sp.dma_start(self.stack[0][b][self.KM + r:self.KM + r + 1, :].rearrange("p (t q) -> p t q", q=P),
                         self.mparts[0:NT, r, :]).then_inc(self.rows_in, 16)

    def scalar_prepare(self, nc, act, s, n):
        if n != V_AT:
            return
        hp, b = s + 1, 1 - self.par
        if isinstance(s, int) and s < 0:
            act.wait_ge(self.vproj_taken, NC)
            act.wait_ge(self.consts, 1)
        else:
            act.wait_ge(self.pv_done, s * NU + NB)
        nc.scalar.activation(self.vf[b][:, :, 0:DA], self.vwhole[:, :, bass.ds(hp * DA, DA)], ACT.Copy)
        nc.scalar.activation(
            self.v[b][:, :, 0:2 * DA],
            self.vall[:, :, :, :, :].rearrange("p t h c d -> p t (h c d)")
                [:, :, bass.ds(hp * 2 * DA, 2 * DA)].bitcast(F32), ACT.Copy).then_inc(self.v_ready, 1)

    def tensor_prepare(self, nc, pe, s, n):
        pass

    def wait_operands(self, pe, hp, c):
        if c == 0:
            pe.wait_ge(self.staged, self.STAGE * (hp + 1))

    def wait_turn_bank(self, pe, hp):
        pass

    def wait_values(self, pe, s):
        pe.wait_ge(self.v_ready, s + 1)

    def take_rows(self, nc, dve, hp):
        m, mp = self.mrow[0:NT], self.mparts[0:NT]
        steps = [lambda: nc.vector.tensor_copy(m[:, 0, :], self.aux[0:NT, 0:P]),
                 lambda: nc.vector.tensor_copy(mp[:, 0, :], m[:, 0, :]),
                 lambda: nc.vector.tensor_tensor(m[:, 1, :], m[:, 0, :], mp[:, 0, :], ALU.subtract),
                 lambda: nc.vector.tensor_copy(mp[:, 1, :], m[:, 1, :]),
                 lambda: nc.vector.tensor_tensor(m[:, 2, :], m[:, 1, :], mp[:, 1, :], ALU.subtract)]
        for i, step in enumerate(steps):
            step().then_inc(self.row_own, 1)
            dve.wait_ge(self.row_own, hp * len(steps) + i + 1)
        nc.vector.tensor_copy(mp[:, 2, :], m[:, 2, :]).then_inc(self.mt_taken, 1)


class AttentionB(Attention):
    D = DB
    ROWS = 16 * 2
    WEIGHTS_AT = 33
    GROUPS = 3 * NC
    AT = [0, 1, 2, 5, 8, 11, 14, 17, 20, 23, 27, 31]
    FIRST_MAX, END_MAX, TURN = 5, 35, 35
    LO_LAG = 3
    SPLIT = list(range(NU))
    LO_ON_POOL = [n for n in range(NU) if n % 3 != 1]

    def __init__(self, name, sem, g, sb):
        super().__init__(name, sem, g)
        self.att = sb("b_att", [P, 2, TPC, DB], F32)
        self.xnT, self.latT = ([sb(f"b_{x}{i}", [P, T], F32R) for i in range(2)] for x in ("xnT", "latT"))
        self.wdown = sb("b_wdown", [P, 2, P], F32R)
        self.wh = sb("b_wh", [P, 4 * DB], F32)
        self.wp = sb("b_wp", [P, 2, 2, 4 * DB], F32R)
        self.kvT = sb("b_kvT", [P, T], F32)
        self.v1 = [sb(f"b_v1{i}", [P, NT, self.VM], F32R) for i in range(2)]
        self.v2 = [sb(f"b_v2{i}", [P, NT, self.VM], F32R) for i in range(2)]
        self.mrow = sb("b_mrow", [P, 2, P], F32R)
        self.q1, self.q2, self.k1, self.k2 = ([sb(f"b_{x}{i}", [P, T], F32R) for i in range(2)]
                                              for x in ("q1", "q2", "k1", "k2"))
        R = DB + 2
        self.main_pairs = [[(self.k1[i][:, :], self.q1[i][:, :]),
                            (self.k2[i][0:R], self.q2[i][0:R])] for i in range(2)]
        self.q_max, self.k_max = self.q1, self.k1
        self.down_hi = sem(f"{name}_down_hi")
        self.lat_ready = sem(f"{name}_lat_ready")
        self.lat_taken = sem(f"{name}_lat_taken")
        self.wh_in = sem(f"{name}_wh_in")
        self.wh_hi = sem(f"{name}_wh_hi")
        self.wh_split = sem(f"{name}_wh_split")
        self.lat_hi = sem(f"{name}_lat_hi")
        self.proj_ready = sem(f"{name}_proj_ready")
        self.proj_hi = sem(f"{name}_proj_hi")
        self.proj_taken = sem(f"{name}_proj_taken")
        self.stored = [sem(f"{name}_stored{i}") for i in range(2)]

    def att_out(self, s, j):
        return self.att[:, j % 2, :, :]

    def wait_att(self, dve, s, j):
        dve.wait_ge(self.stored[j % 2], (s * (NC // 2) + j // 2 + 1) * 16)

    def value_products(self, b, kt, hi, lo):
        v1, v2 = self.v1[b][:, kt, :], self.v2[b][:, kt, :]
        return [(v1, hi), (v1, lo), (v2, hi)]

    def sums_and_values(self, nc):
        return self.tr[:, :, DB], self.tr[:, :, 0:DB]

    def product(self, nc, out, w, x):
        parts = [(0, 0), (0, 1), (1, 0)]
        for i, (a, b) in enumerate(parts):
            mm = nc.tensor.matmul(out, w[a], x[b], start=i == 0, stop=i == len(parts) - 1)
        return mm

    def scalar_weights(self, nc, act, h, b):
        act.wait_ge(self.wh_in, 16 * (h + 1))
        nc.scalar.activation(self.wp[:, b, 0, :], self.wh[:, :], ACT.Copy).then_inc(self.wh_hi, 1)

    def vector_weights(self, nc, dve, h, b):
        dve.wait_ge(self.wh_hi, h + 1)
        nc.vector.tensor_tensor(self.wp[:, b, 1, :], self.wh[:, :], self.wp[:, b, 0, :].bitcast(F32),
                                ALU.subtract).then_inc(self.wh_split, 1)

    def tensor_project(self, nc, pe, ln):
        g = self.g
        pe.wait_ge(ln.xT_ready, NC)
        pe.wait_ge(self.consts, 1)
        for c in range(NC):
            if c >= 2:
                pe.wait_ge(self.lat_taken, c - 1)
            self.product(nc, g.bank[c % 2][:, :], [self.wdown[:, i, :] for i in range(2)],
                         [x[:, c * C:(c + 1) * C] for x in self.xnT]).then_inc(self.lat_ready, 1)
        pe.wait_ge(self.lat_taken, NC)

    def scalar_project(self, nc, act):
        g = self.g
        for c in range(NC):
            act.wait_ge(self.lat_ready, c + 1)
            nc.scalar.activation(self.latT[0][:, c * C:(c + 1) * C], g.bank[c % 2][:, :], ACT.Copy)\
                .then_inc(self.lat_hi, 1)
        act.wait_ge(self.consts, 1)

    def vector_project(self, nc, dve):
        for i in range(2):
            nc.vector.memset(self.k2[i][DB:DB + 2, :].bitcast(F32), 1.0)
            nc.vector.memset(self.v1[i][:, :, DB:].bitcast(F32), 1.0)
            nc.vector.memset(self.v2[i][:, :, DB:].bitcast(F32), 0.0)
        nc.vector.memset(self.g.mpart, LOWEST)
        nc.vector.tensor_copy(self.wdown[:, 0, :], self.g.wdown).then_inc(self.down_hi, 1)
        dve.wait_ge(self.down_hi, 1)
        nc.vector.tensor_tensor(self.wdown[:, 1, :], self.g.wdown, self.wdown[:, 0, :].bitcast(F32),
                                ALU.subtract).then_inc(self.consts, 1)
        dve.wait_ge(self.consts, 1)
        for c in range(NC):
            cols = slice(c * C, (c + 1) * C)
            dve.wait_ge(self.lat_hi, c + 1)
            nc.vector.tensor_tensor(self.latT[1][:, cols], self.g.bank[c % 2][:, :],
                                    self.latT[0][:, cols].bitcast(F32), ALU.subtract)\
                .then_inc(self.lat_taken, 1)

    def vector_credits(self, nc):
        super().vector_credits(nc)
        nc.vector.sem_inc(self.proj_taken, 1)

    def group(self, n):
        k = self.AT.index(n)
        c, which = divmod(k, 2) if k < 2 * NC else (k - 2 * NC, 2)
        return k, which, c, self.sm[k] if k < 2 else self.aux

    def turned_values(self, bank):
        return bank[:, :].rearrange("p (t d) -> p t d", d=P)[:, :, DB:P]

    def sync_step(self, nc, sp, s, main, prep, before):
        g = self.g
        hp, b = s + 1, 1 - self.par
        if prep:
            for h in ([0, 1] if not main else [hp + 1]):
                if not isinstance(h, int) or h > 0:
                    sp.wait_ge(self.wh_split, h)
                sp.dma_start(self.wh[:, :].unsqueeze(1), g.w_heads[:, bass.ds(h, 1), :])\
                    .then_inc(self.wh_in, 16)
        if before:
            self.store_chunk(sp, s - 1, NC - 1)
        for j in range(NC - 1):
            if main:
                self.store_chunk(sp, s, j)
            if j == NC - 2 and prep:
                sp.wait_ge(self.mt_taken, hp + 2)
                for r in range(2):
                    sp.dma_start(self.q2[b][DB + r:DB + r + 1, :].bitcast(F32)
                                     .rearrange("p (t q) -> p t q", q=P),
                                 self.mrow[0:NT, r, :].bitcast(F32)).then_inc(self.rows_in, 16)

    def store_chunk(self, sp, s, j):
        sp.wait_ge(self.norm_done, s * NC + j + 3)
        sp.dma_start(self.g.att_dram[:, TPC * j:TPC * (j + 1), bass.ds(s * DB, DB)],
                     self.att[:, j % 2, :, :]).then_inc(self.stored[j % 2], 16)

    def tensor_prepare(self, nc, pe, s, n):
        if n not in self.AT:
            return
        g, hp, b = self.g, s + 1, 1 - self.par
        k, which, c, out = self.group(n)
        if k == 0:
            pe.wait_ge(self.wh_split, hp + 1)
            pe.wait_ge(self.mx_done, hp * NP + 2)
        if k == 2:
            pe.wait_ge(self.mt_taken, hp + 1)
        if k > 2:
            pe.wait_ge(self.proj_taken, hp * self.GROUPS + k + 1)
        if which < 2:
            mm = self.product(nc, out[:, :],
                              [self.wp[:, b, i, which * 2 * DB:(which + 1) * 2 * DB] for i in range(2)],
                              [x[:, c * C:(c + 1) * C] for x in (self.xnT, self.latT)[which]])
        else:
            for t in range(TPC):
                mm = nc.tensor.transpose(out[:, t * P:(t + 1) * P],
                                         self.kvT[:, (c * TPC + t) * P:(c * TPC + t + 1) * P], g.ident)
        mm.then_inc(self.proj_ready, 1)

    def scalar_prepare(self, nc, act, s, n):
        if n == self.WEIGHTS_AT:
            if isinstance(s, int) and s < 0:
                self.scalar_weights(nc, act, 1, 1)
            else:
                self.scalar_weights(nc, act, s + 2, self.par)
        if n not in self.AT:
            return
        hp, b = s + 1, 1 - self.par
        k, which, c, bank = self.group(n)
        cols = slice(c * C, (c + 1) * C)
        act.wait_ge(self.proj_ready, hp * self.GROUPS + k + 1)
        if which == 0:
            nc.scalar.activation(self.q1[b][:, cols], bank[:, :], ACT.Copy)
            ins = nc.scalar.activation(self.q2[b][0:DB, cols], bank[0:DB, :], ACT.Copy)
        elif which == 1:
            nc.scalar.activation(self.kvT[:, cols], bank[:, :], ACT.Copy)
            nc.scalar.activation(self.k1[b][0:DB, cols], bank[0:DB, :], ACT.Copy)
            ins = nc.scalar.activation(self.k1[b][DB:P, cols], bank[0:DB, :], ACT.Copy)
        else:
            ins = nc.scalar.activation(self.v1[b][:, c * TPC:(c + 1) * TPC, 0:DB],
                                       self.turned_values(bank), ACT.Copy)
        ins.then_inc(self.proj_hi, 1)

    def vector_prepare(self, nc, dve, s, n):
        if n == self.WEIGHTS_AT:
            if isinstance(s, int) and s < 0:
                self.vector_weights(nc, dve, 1, 1)
            else:
                self.vector_weights(nc, dve, s + 2, self.par)
        if n not in self.AT:
            return
        hp, b = s + 1, 1 - self.par
        k, which, c, bank = self.group(n)
        cols = slice(c * C, (c + 1) * C)
        dve.wait_ge(self.proj_hi, hp * self.GROUPS + k + 1)
        if which == 0:
            out, x, hi = self.q1[b][DB:P, cols], bank[DB:P, :], self.q1[b][DB:P, cols]
        elif which == 1:
            out, x, hi = self.k2[b][0:DB, cols], bank[0:DB, :], self.k1[b][0:DB, cols]
        else:
            tiles = slice(c * TPC, (c + 1) * TPC)
            out, hi = self.v2[b][:, tiles, 0:DB], self.v1[b][:, tiles, 0:DB]
            x = self.turned_values(bank)
        nc.vector.tensor_tensor(out, x, hi.bitcast(F32), ALU.subtract).then_inc(self.proj_taken, 1)

    def wait_operands(self, pe, hp, c):
        pe.wait_ge(self.proj_taken, hp * self.GROUPS + 2 * (c + 1) + 1)

    def wait_turn_bank(self, pe, hp):
        pe.wait_ge(self.proj_taken, (hp + 1) * self.GROUPS + 1)

    def wait_values(self, pe, s):
        pe.wait_ge(self.proj_taken, (s + 1) * self.GROUPS + 1)

    def take_rows(self, nc, dve, hp):
        m, mt = self.mrow[0:NT], self.aux[0:NT, 0:P]
        nc.vector.tensor_copy(m[:, 0, :], mt).then_inc(self.row_own, 1)
        dve.wait_ge(self.row_own, hp + 1)
        nc.vector.tensor_tensor(m[:, 1, :], mt, m[:, 0, :].bitcast(F32), ALU.subtract)\
            .then_inc(self.mt_taken, 1)


class OutProj:

    def __init__(self, name, sem, g, rows, cols, KT, att, w, bias, done):
        self.g, self.KT, self.att, self.w, self.bias = g, KT, att, w, bias
        self.done = done
        self.rows, self.cols = rows, cols
        self.staged = [sem(f"{name}_staged{i}") for i in range(2)]
        self.turned = sem(f"{name}_turned")
        self.taken = sem(f"{name}_taken")
        self.y_ready = sem(f"{name}_y_ready")
        self.added = sem(f"{name}_added")
        self.bias_own = sem(f"{name}_bias_own")
        B = g.bank
        self.tb = [B[0:2], B[2:4]]
        self.yb = B[4:6]

    def run(self, eng, first, second):
        first(0, 0, 0)
        with eng.Fori(0, NT // 2 - 1) as u:
            first(u * 2 + 1, 1, u)
            second(u * 2, 0)
            first(u * 2 + 2, 0, u + 1)
            second(u * 2 + 1, 1)
        first(NT - 1, 1, NT // 2 - 1)
        second(NT - 2, 0)
        second(NT - 1, 1)

    UNIT = 1

    def sync(self, sp):
        self.UNIT = 16
        for what, count in self.done:
            sp.wait_ge(what, count)

        def stage(t, b, half):
            sp.wait_ge(self.turned, t + 1)
            sp.dma_start(self.rows[:, b, :].unsqueeze(1), self.att[:, bass.ds(t, 1), :])\
                .then_inc(self.staged[b], 16)
        self.run(sp, stage, lambda t, b: None)

    def scalar(self, nc, act):
        for what, count in self.done:
            act.wait_ge(what, count)

        def stage(t, b, half):
            act.wait_ge(self.turned, t + 1)
            nc.scalar.activation(self.rows[:, b, :], self.att[:, bass.ds(t, 1), :], ACT.Copy)\
                .then_inc(self.staged[b], 1)
        self.run(act, stage, lambda t, b: None)

    def tensor(self, nc, pe):
        nc.tensor.sem_inc(self.turned, 2)
        nc.tensor.sem_inc(self.y_ready, 2)

        def turn(t, b, half):
            pe.wait_ge(self.staged[b], (half + 1) * self.UNIT)
            pe.wait_ge(self.taken, t + 1)
            for k in range(self.KT):
                mm = nc.tensor.transpose(self.tb[b][k // TPC][:, k % TPC * P:(k % TPC + 1) * P],
                                         self.rows[:, b, k * P:(k + 1) * P], self.g.ident)
            mm.then_inc(self.turned, 1)

        def product(t, b):
            pe.wait_ge(self.taken, t + 3)
            pe.wait_ge(self.added, t + 1)
            for k in range(self.KT):
                mm = nc.tensor.matmul(self.yb[b][:, 0:E], self.cols[:, b, k * P:(k + 1) * P],
                                      self.w[:, k, :], start=k == 0, stop=k == self.KT - 1)
            mm.then_inc(self.y_ready, 1)
        self.run(pe, turn, product)

    def vector(self, nc, dve):
        g = self.g
        nc.vector.sem_inc(self.taken, 2)
        nc.vector.sem_inc(self.added, 2)

        def take(t, b, half):
            dve.wait_ge(self.turned, t + 3)
            dve.wait_ge(self.y_ready, t + 1)
            halves = range(0, self.KT, TPC)
            for k in halves:
                w = min(self.KT - k, TPC) * P
                ins = nc.vector.tensor_copy(self.cols[:, b, k * P:k * P + w], self.tb[b][k // TPC][:, 0:w])
            ins.then_inc(self.taken, 1)

        def add(t, b):
            dve.wait_ge(self.y_ready, t + 3)
            if self.bias is not None:
                nc.vector.tensor_tensor(g.x[:, bass.ds(t, 1), :], g.x[:, bass.ds(t, 1), :],
                                        self.bias.unsqueeze(1), ALU.add).then_inc(self.bias_own, 1)
                dve.wait_ge(self.bias_own, t + 1)
            nc.vector.tensor_tensor(g.x[:, bass.ds(t, 1), :], self.yb[b][:, 0:E].unsqueeze(1),
                                    g.x[:, bass.ds(t, 1), :], ALU.add).then_inc(self.added, 1)
        self.run(dve, take, add)
        dve.wait_ge(self.added, NT + 2)


class TreeFFN:

    def __init__(self, name, sem, g, sb):
        self.g = g
        self.act = sb(f"{name}_act", [P, 2, 2, C], F32)
        self.msk = sb(f"{name}_msk", [P, 2, 2, C], F32)
        self.mparts = [part[:, 0:4, :].rearrange("p (b l) c -> p b l c", l=2) for part in (g.hi, g.lo)]
        self.xnT = [sb(f"{name}_xnT{i}", [P, T], F32R) for i in range(2)]
        self.win = [sb(f"{name}_win{i}", [P, 2 * TREES, P], F32R) for i in range(2)]
        self.wout = [sb(f"{name}_wout{i}", [P, 2 * TREES, E], F32R) for i in range(2)]
        self.dec = sb(f"{name}_dec", [P, 2, C], BF16)
        B = g.bank
        self.lg = [B[0:2], B[2:4]]
        self.cnt = B[4:6]
        self.y, self.yt = B[6], B[7]
        self.yrow = sb(f"{name}_yrow", [P, C], F32)
        self.lg_ready = sem(f"{name}_lg_ready")
        self.silu_done = sem(f"{name}_silu_done")
        self.dec_done = sem(f"{name}_dec_done")
        self.cnt_ready = sem(f"{name}_cnt_ready")
        self.mask_done = sem(f"{name}_mask_done")
        self.w_hi = sem(f"{name}_w_hi")
        self.w_lo = sem(f"{name}_w_lo")
        self.m_hi = sem(f"{name}_m_hi")
        self.m_lo = sem(f"{name}_m_lo")
        self.out_done = sem(f"{name}_out_done")
        self.y_taken = sem(f"{name}_y_taken")
        self.y_turned = sem(f"{name}_y_turned")
        self.added = sem(f"{name}_added")

    def run(self, eng, step):
        step(0, True, False)
        with eng.Fori(0, NC - 1) as u:
            step(u + 1, True, True)
        step(NC, False, True)

    def trees(self, c, main, before, stages):
        per_tree, per_chunk = stages
        for p in range(TREES):
            for lag, do in per_tree:
                if main and p >= lag or before and p < lag:
                    do(c * TREES + (p - lag), (p - lag) % TREES, c)
            for lag, do in per_chunk:
                if before and p == lag - TREES:
                    do(c - 1)

    def tensor(self, nc, pe, ln):
        g = self.g
        nc.tensor.sem_inc(self.cnt_ready, 4)
        nc.tensor.sem_inc(self.out_done, 2)
        pe.wait_ge(ln.xT_ready, NC)
        pe.wait_ge(self.w_lo, 2)
        parts = [(0, 0), (0, 1), (1, 0)]

        def logits(G, p, c):
            pe.wait_ge(self.silu_done, G * 2 + 2)
            pe.wait_ge(self.dec_done, G + 1)
            for leaf in range(2):
                for i, (w, m) in enumerate(parts):
                    mm = nc.tensor.matmul(self.lg[p % 2][leaf][:, :], self.win[w][:, 2 * p + leaf, :],
                                          self.xnT[m][:, bass.ds(c * C, C)],
                                          start=i == 0, stop=i == len(parts) - 1)
                mm.then_inc(self.lg_ready, 1)

        def paths(G, p, c):
            pe.wait_ge(self.dec_done, G + 3)
            pe.wait_ge(self.mask_done, G * 2 + 4)
            for leaf in range(2):
                nc.tensor.matmul(self.cnt[leaf][:, :], g.anc[:, leaf, :], self.dec[:, p % 2, :],
                                 start=True, stop=True).then_inc(self.cnt_ready, 1)

        def output(G, p, c):
            if p == 0:
                pe.wait_ge(self.y_taken, c + 1)
            for leaf in range(2):
                pe.wait_ge(self.m_lo, G * 2 + leaf + 5)
                for i, (w, m) in enumerate(parts):
                    mm = nc.tensor.matmul(self.y[:, :], self.wout[w][:, 2 * p + leaf, :],
                                          self.mparts[m][:, p % 2, leaf, :],
                                          start=p == 0 and leaf == 0 and i == 0,
                                          stop=p == TREES - 1 and leaf == 1 and i == len(parts) - 1)
            mm.then_inc(self.out_done, 1)

        def turn(c):
            pe.wait_ge(self.y_taken, c + 2)
            pe.wait_ge(self.added, c + 1)
            for t in range(TPC):
                mm = nc.tensor.transpose(self.yt[:, t * P:(t + 1) * P], self.yrow[:, t * P:(t + 1) * P],
                                         g.ident)
            mm.then_inc(self.y_turned, 1)
        self.run(pe, lambda *a: self.trees(*a, ([(0, logits), (1, paths), (3, output)],
                                                [(TREES + 4, turn)])))

    def scalar(self, nc, act):
        g = self.g
        nc.scalar.sem_inc(self.silu_done, 4)
        nc.scalar.sem_inc(self.y_taken, 1)

        def silu(G, p, c):
            act.wait_ge(self.mask_done, G * 2 + 2)
            for leaf in range(2):
                act.wait_ge(self.lg_ready, G * 2 + leaf + 1)
                nc.scalar.activation(self.act[:, p % 2, leaf, :], self.lg[p % 2][leaf][:, :],
                                     ACT.Silu, bias=g.bin[:, 2 * p + leaf:2 * p + leaf + 1])\
                    .then_inc(self.silu_done, 1)

        def hi_part(G, p, c):
            act.wait_ge(self.out_done, G + 1)
            for leaf in range(2):
                act.wait_ge(self.mask_done, G * 2 + leaf + 5)
                nc.scalar.activation(self.mparts[0][:, p % 2, leaf, :], self.msk[:, p % 2, leaf, :],
                                     ACT.Copy).then_inc(self.m_hi, 1)

        def take(c):
            act.wait_ge(self.out_done, c * TREES + TREES + 2)
            nc.scalar.activation(self.yrow[:, :], self.y[:, :], ACT.Copy).then_inc(self.y_taken, 1)
        self.run(act, lambda *a: self.trees(*a, ([(0, silu), (2, hi_part)], [(TREES + 2, take)])))

    def scalar_weights(self, nc, act):
        g = self.g
        for whole, parts in ((g.win, self.win), (g.wout, self.wout)):
            nc.scalar.activation(parts[0][:, :, :], whole[:, :, :], ACT.Copy).then_inc(self.w_hi, 1)

    def gpsimd(self, nc, pool):
        g = self.g
        for i, (whole, parts) in enumerate(((g.win, self.win), (g.wout, self.wout))):
            pool.wait_ge(self.w_hi, i + 1)
            nc.gpsimd.tensor_tensor(parts[1][:, :, :], whole[:, :, :], parts[0][:, :, :].bitcast(F32),
                                    ALU.subtract).then_inc(self.w_lo, 1)
        nc.gpsimd.sem_inc(self.m_lo, 4)
        with pool.Fori(0, NC) as c:
            for q in range(TREES):
                G = c * TREES + q
                for leaf in range(2):
                    pool.wait_ge(self.m_hi, G * 2 + leaf + 1)
                    nc.gpsimd.tensor_tensor(self.mparts[1][:, q % 2, leaf, :], self.msk[:, q % 2, leaf, :],
                                            self.mparts[0][:, q % 2, leaf, :].bitcast(F32), ALU.subtract)\
                        .then_inc(self.m_lo, 1)

    def vector(self, nc, dve):
        g = self.g
        nc.vector.sem_inc(self.dec_done, 2)
        nc.vector.sem_inc(self.mask_done, 4)
        nc.vector.sem_inc(self.added, 1)

        def decide(G, p, c):
            dve.wait_ge(self.silu_done, G * 2 + 5)
            dve.wait_ge(self.cnt_ready, G * 2 + 2)
            nc.vector.tensor_scalar(self.dec[:, p % 2, :], self.lg[p % 2][0][:, :],
                                    g.bin[:, 2 * p:2 * p + 1], 0.0, ALU.add, ALU.is_gt)\
                .then_inc(self.dec_done, 1)

        def mask(G, p, c):
            dve.wait_ge(self.silu_done, G * 2 + 6)
            dve.wait_ge(self.m_lo, G * 2 + 2)
            for leaf in range(2):
                dve.wait_ge(self.cnt_ready, G * 2 + 5 + leaf)
                nc.vector.scalar_tensor_tensor(
                    out=self.msk[:, p % 2, leaf, :], in0=self.cnt[leaf][:, :],
                    scalar=g.nright[:, leaf:leaf + 1], in1=self.act[:, p % 2, leaf, :],
                    op0=ALU.is_equal, op1=ALU.mult).then_inc(self.mask_done, 1)

        def add(c):
            dve.wait_ge(self.y_turned, c + 1)
            nc.vector.tensor_tensor(g.x[:, bass.ds(c * TPC, TPC), :],
                                    self.yt[:, :].rearrange("p (t e) -> p t e", e=E),
                                    g.x[:, bass.ds(c * TPC, TPC), :], ALU.add).then_inc(self.added, 1)
        self.run(dve, lambda *a: self.trees(*a, ([(0, decide), (1, mask)], [(TREES + 5, add)])))
        dve.wait_ge(self.added, NC + 1)


class Shared:
    pass


def hybrid_kernel(nc, t, out):
    with ExitStack() as ctx:
        def sb(name, shape, dt):
            return ctx.enter_context(nc.sbuf_tensor(name, shape, dt))

        def sem(name):
            return ctx.enter_context(nc.semaphore(name))

        g = Shared()
        g.bank = [ctx.enter_context(nc.psum_tensor(f"bank{i}", [P, C], F32)) for i in range(8)]
        g.w_heads = t["w_heads"]

        x = sb("x", [P, NT, E], F32)
        win = sb("win", [P, 2 * TREES, P], F32)
        wout = sb("wout", [P, 2 * TREES, E], F32)
        wob = sb("wob", [P, H * DB // P, E], F32)
        wa = sb("wa", [P, 5, E], F32)
        wdown = sb("wdown", [P, P], F32)
        wproj = sb("wproj", [P, 1, E], F32)
        ba = sb("ba", [P, 4], F32)
        bv = sb("bv", [P, E], F32)
        bproj = sb("bproj", [P, E], F32)
        bin_ = sb("bin", [P, 2 * TREES], F32)
        ident = sb("ident", [P, P], F32)
        identb = sb("identb", [P, P], BF16)
        masks = sb("masks", [P, 2, P], BF16)
        anc = sb("anc", [P, 2, P], BF16)
        nright = sb("nright", [P, 2], F32)
        stats = sb("stats", [P, NT, 6], F32)
        mv = sb("mv", [P, NT, 2], F32)
        ve = sb("ve", [P, NT], F32)
        std = sb("std", [P, NT], F32)
        rstd = sb("rstd", [P, NT], F32)
        mpart = sb("mpart", [P, NT, NC], F32)
        negm = sb("negm", [P, NT], F32)
        rcp = sb("rcp", [P, 2, TPC], F32)
        pb = sb("pb", [P, NB, C], F32)
        hi = sb("hi", [P, NB, C], F32R)
        lo = sb("lo", [P, NB, C], F32R)
        ot = sb("ot", [P, 2, C], F32)
        xn = sb("xn", [P, 2, C], F32)
        g.x, g.win, g.wout, g.wa, g.wdown = x, win, wout, wa, wdown[:, :]
        g.ba, g.bv, g.bin = ba, bv[:, :], bin_
        g.ident, g.identb, g.mask_kq, g.mask_qk = ident[:, :], identb[:, :], masks[:, 0, :], masks[:, 1, :]
        g.anc, g.nright, g.stats, g.mv = anc, nright, stats, mv
        g.ve, g.std, g.rstd = ve[:, :], std[:, :], rstd[:, :]
        g.mpart, g.negm, g.rcp, g.pb = mpart[:, :, :], negm[:, :], rcp, pb
        g.hi, g.lo, g.ot, g.xn = hi, lo, ot, xn
        g.spill = nc.dram_tensor("qk_stacks", (2, len(PAIRS), E, T), BF16, kind="Internal").ap()
        g.att_dram = nc.dram_tensor("att_b", (T, H * DB), F32, kind="Internal").ap()\
            .rearrange("(t p) c -> p t c", p=P)

        g.x_in = sem("x_in")
        g.w_in = sem("w_in")
        g.w_late = sem("w_late")
        g.stored = sem("stored")
        first = [(ident[:, :], t["ident"]), (wa[:, :, :], t["wa"]), (ba[:, :], t["ba"]), (bv[:, :], t["bv"]),
                 (identb[:, :], t["identb"]), (masks[:, :, :], t["masks"])]
        later = [(wproj[:, 0, :], t["wproj"]), (bproj[:, :], t["bproj"]),
                 (win[:, :, :], t["win"]), (wout[:, :, :], t["wout"]), (bin_[:, :], t["bin"]),
                 (anc[:, :, :], t["anc"]), (nright[:, :], t["nright"]),
                 (wdown[:, :], t["w_down"]), (wob[:, :, :], t["w_out"])]

        ln = [Norm(f"ln{i}", sem, g) for i in range(4)]

        with ExitStack() as own:
            def sb(name, shape, dt):
                return own.enter_context(nc.sbuf_tensor(name, shape, dt))
            g.xnT = xnT = sb("xnT", [P, T], F32)
            att = AttentionA("a", sem, g, sb)
            proj = OutProj("pa", sem, g, sb("pa_rows", [P, 2, P], F32), sb("pa_cols", [P, 2, P], F32), 1, att.att, wproj, bproj[:, :], [(att.norm_done, H * NC + 2)])
            block = own.enter_context(nc.Block())

            @block.sync
            def _(sp):
                sp.dma_start(x[:, :, :], t["x"][0].rearrange("(t p) e -> p t e", p=P)).then_inc(g.x_in, 16)
                for dst, src in first:
                    sp.dma_start(dst, src).then_inc(g.w_in, 16)
                sp.dma_start(att.tables[:, 0, :], t["cos"]).then_inc(att.tables_in, 16)
                sp.dma_start(att.tables[:, 1, :], t["sin"]).then_inc(att.tables_in, 16)
                for dst, src in later:
                    sp.dma_start(dst, src).then_inc(g.w_late, 16)
                sp.sem_inc(att.rows_in, att.ROWS)
                sp.wait_ge(att.consts, 1)
                att.sync_spill(sp)
                att.run(sp, lambda *a: att.sync_step(nc, sp, *a))
                sp.wait_ge(g.w_late, 16 * len(later))

            @block.vector
            def _(dve):
                dve.wait_ge(g.x_in, 16)
                ln[0].vector(nc, dve, [xnT])
                dve.wait_ge(g.w_in, 16 * len(first))
                att.vector_credits(nc)
                att.vector_project(nc, dve)
                att.run(dve, lambda *a: att.vector_step(nc, dve, *a))
                att.vector_end(nc, dve)
                proj.vector(nc, dve)

            @block.gpsimd
            def _(pool):
                att.run(pool, lambda *a: att.pool_step(nc, pool, *a))

            @block.scalar
            def _(act):
                ln[0].scalar(nc, act, [xnT])
                att.scalar_project(nc, act)
                att.scalar_credits(nc)
                att.run(act, lambda *a: att.scalar_step(nc, act, *a))
                att.scalar_end(nc, act)
                proj.scalar(nc, act)

            @block.tensor
            def _(pe):
                pe.wait_ge(g.w_in, 16 * len(first))
                ln[0].tensor(nc, pe)
                att.tensor_credits(nc)
                att.tensor_project(nc, pe, ln[0])
                att.run(pe, lambda *a: att.tensor_step(nc, pe, *a))
                att.tensor_end(nc, pe)
                pe.wait_ge(g.w_late, 16 * len(later))
                proj.tensor(nc, pe)

        def feed_forward(i, norm):
            with ExitStack() as own:
                def sb(name, shape, dt):
                    return own.enter_context(nc.sbuf_tensor(name, shape, dt))
                ffn = TreeFFN(f"f{i}", sem, g, sb)
                block = own.enter_context(nc.Block())

                @block.vector
                def _(dve):
                    norm.vector(nc, dve, ffn.xnT)
                    ffn.vector(nc, dve)

                @block.scalar
                def _(act):
                    ffn.scalar_weights(nc, act)
                    norm.scalar(nc, act, ffn.xnT)
                    ffn.scalar(nc, act)

                @block.tensor
                def _(pe):
                    norm.tensor(nc, pe)
                    ffn.tensor(nc, pe, norm)

                @block.gpsimd
                def _(pool):
                    ffn.gpsimd(nc, pool)

                @block.sync
                def _(sp):
                    if i == 1:
                        sp.wait_ge(ffn.added, NC + 1)
                        sp.dma_start(out[0].rearrange("(t p) e -> p t e", p=P), x[:, :, :])\
                            .then_inc(g.stored, 16)
                        sp.wait_ge(g.stored, 16)

        feed_forward(0, ln[1])

        with ExitStack() as own:
            def sb(name, shape, dt):
                return own.enter_context(nc.sbuf_tensor(name, shape, dt))
            att_b = AttentionB("b", sem, g, sb)
            proj_b = OutProj("pb", sem, g, pb[:, 0:4, :].rearrange("p (b k) c -> p b (k c)", b=2),
                             att_b.kvT[:, :].rearrange("p (b c) -> p b c", b=2), H * DB // P, g.att_dram, wob, None,
                             [(done, 16 * (H * NC // 2 + 1)) for done in att_b.stored])
            block = own.enter_context(nc.Block())

            @block.sync
            def _(sp):
                sp.sem_inc(att_b.rows_in, att_b.ROWS)
                for done in att_b.stored:
                    sp.sem_inc(done, 16)
                sp.wait_ge(att_b.consts, 1)
                att_b.run(sp, lambda *a: att_b.sync_step(nc, sp, *a))
                att_b.store_chunk(sp, H - 1, NC - 1)
                proj_b.sync(sp)

            @block.vector
            def _(dve):
                ln[2].vector(nc, dve, att_b.xnT)
                att_b.vector_credits(nc)
                att_b.vector_project(nc, dve)
                att_b.vector_weights(nc, dve, 0, 0)
                att_b.run(dve, lambda *a: att_b.vector_step(nc, dve, *a))
                att_b.vector_end(nc, dve)
                proj_b.vector(nc, dve)

            @block.gpsimd
            def _(pool):
                att_b.run(pool, lambda *a: att_b.pool_step(nc, pool, *a))

            @block.scalar
            def _(act):
                ln[2].scalar(nc, act, att_b.xnT)
                att_b.scalar_credits(nc)
                att_b.scalar_project(nc, act)
                att_b.scalar_weights(nc, act, 0, 0)
                att_b.run(act, lambda *a: att_b.scalar_step(nc, act, *a))
                att_b.scalar_end(nc, act)

            @block.tensor
            def _(pe):
                ln[2].tensor(nc, pe)
                att_b.tensor_credits(nc)
                att_b.tensor_project(nc, pe, ln[2])
                att_b.run(pe, lambda *a: att_b.tensor_step(nc, pe, *a))
                att_b.tensor_end(nc, pe)
                proj_b.tensor(nc, pe)

        feed_forward(1, ln[3])


def rope_tables(np):
    pos = np.arange(T, dtype=np.float32)
    inv = (1.0 / np.float32(10000.0) ** (np.arange(0, DA, 2, dtype=np.float32) / np.float32(DA))).astype(np.float32)
    freqs = inv[:, None] * pos[None, :]
    cos = np.repeat(np.cos(freqs), 2, axis=0)
    sin = np.repeat(np.sin(freqs), 2, axis=0) * np.tile(np.array([-1.0, 1.0], np.float32), DA // 2)[:, None]
    return (np.ascontiguousarray(np.tile(a, (H, 1)).astype(np.float32)) for a in (cos, sin))


def tree_tables(np):
    inner = 2 ** DEPTH - 1
    anc = np.zeros((P, 2, P), np.float32)
    right = np.zeros((P, 2), np.float32)
    for node in range(2 * inner + 1):
        leaf, col = (0, node) if node < inner else (1, node - inner)
        at = node
        while at > 0:
            up, step = (at - 1) // 2, 1 if at % 2 == 0 else -1
            anc[up, leaf, col] = step
            right[col, leaf] += step == 1
            at = up
    return anc, right


def kernel(**inputs):
    import numpy as np
    import ml_dtypes
    import concourse.bacc as bacc
    from concourse.bass_utils import run_bass_kernel_spmd as run

    a = {k: np.asarray(v) for k, v in inputs.items()}
    inner, nodes = 2 ** DEPTH - 1, 2 ** (DEPTH + 1) - 1
    bf16 = ml_dtypes.bfloat16
    cos, sin = rope_tables(np)
    anc, right = tree_tables(np)
    turned = np.arange(E) ^ 1
    W, b = a["L0_attn_a_Wqkv"], a["L0_attn_a_bqkv"]
    wq, wk, wv = W[:, :E], W[:, E:2 * E], W[:, 2 * E:]
    bq, bk, bv = b[:E], b[E:2 * E], b[2 * E:]

    def by_tree(w):
        w = w.reshape(TREES, nodes, *w.shape[1:])
        full = np.zeros((P, TREES, 2) + w.shape[2:], w.dtype)
        full[:inner, :, 0] = np.swapaxes(w[:, :inner], 0, 1)
        full[:, :, 1] = np.swapaxes(w[:, inner:], 0, 1)
        return full.reshape((P, 2 * TREES) + w.shape[2:])

    w_heads = np.zeros((P, H + 1, 4, DB), a["L0_attn_b_w_q"].dtype)
    w_q = a["L0_attn_b_w_q"].reshape(P, H, DB)
    w_up = a["L0_attn_b_w_kv_up"].reshape(P, 2, H, DB)
    for i, w in enumerate((w_q, w_q, w_up[:, 0], w_up[:, 1])):
        w_heads[:, :H, i] = w
    rows = np.arange(P)
    masks = np.zeros((P, 2, P), np.float32)
    masks[:, 0][rows[:, None] > rows[None, :]] = NEG
    masks[:, 1][rows[None, :] > rows[:, None]] = NEG
    arrays = {
        "x": a["L0_attn_a_x"],
        "wa": np.stack([wq, wq[:, turned], wk, wk[:, turned], wv], axis=1),
        "ba": np.stack([bq, bq[turned], bk, bk[turned]], axis=1),
        "bv": np.broadcast_to(bv, (P, E)),
        "wproj": a["L0_attn_a_Wproj"],
        "bproj": np.broadcast_to(a["L0_attn_a_bproj"], (P, E)),
        "w_down": a["L0_attn_b_w_kv_down"],
        "w_heads": w_heads.reshape(P, H + 1, 4 * DB),
        "w_out": a["L0_attn_b_w_out"].reshape(H * DB // P, P, E).transpose(1, 0, 2),
        "win": by_tree(a["L0_ffn_W_in"]).transpose(2, 1, 0),
        "bin": by_tree(a["L0_ffn_b_in"]),
        "wout": by_tree(a["L0_ffn_W_out"].T),
        "ident": np.eye(P, dtype=np.float32),
        "identb": np.eye(P, dtype=np.float32).astype(bf16),
        "masks": masks.astype(bf16),
        "anc": anc.astype(bf16),
        "nright": right,
        "cos": cos,
        "sin": sin,
    }
    nc = bacc.Bacc("TRN2", target_bir_lowering=False, num_devices=1)
    arrays = {k: np.ascontiguousarray(v) for k, v in arrays.items()}
    aps = {k: nc.dram_tensor(f"in_{k}", v.shape, mybir.dt.from_np(v.dtype), kind="ExternalInput").ap()
           for k, v in arrays.items()}
    out = nc.dram_tensor("out", (1, T, E), F32, kind="ExternalOutput").ap()
    hybrid_kernel(nc, aps, out)
    r = run(nc, [{f"in_{k}": v for k, v in arrays.items()}], core_ids=[0])
    return r.results[0]["out"]
```
